# Optimizing a Trainium2 kernel written in Bass

```python
import numpy as np
import jax
import jax.numpy as jnp

def _softmax(x, axis=-1):
    return jax.nn.softmax(x, axis=axis)

def _gelu(x):
    return jax.nn.gelu(x, approximate=True)

def _silu(x):
    return jax.nn.silu(x)

def _sigmoid(x):
    return jax.nn.sigmoid(x)

def _layernorm(x, axis=-1, eps=1e-05):
    m = jnp.mean(x, axis=axis, keepdims=True)
    v = jnp.var(x, axis=axis, keepdims=True)
    return (x - m) / jnp.sqrt(v + eps)

def _scatter_add(tgt, idx, src, axis=0):
    return tgt.at[idx].add(src)

def _segment_sum(src, seg, n):
    return jax.ops.segment_sum(src, seg, n)
kernel_name = 'mk_flamingo_gated_d1_seqx_r4_1268f4'

def setup_inputs(seed: int=0):
    np.random.seed(seed)
    _w = jnp.asarray

    def _rec_inputs():
        import jax
        import jax.numpy as jnp
        _rk = jax.random.key(seed)
        x = 0.002226 + 0.9996 * jax.random.normal(jax.random.fold_in(_rk, 1), (32, 112, 256), jnp.float32)
        _lenS = 112 - jax.random.randint(jax.random.fold_in(_rk, 7), (32,), 0, max(1, 112 // 4) + 1, jnp.int32)
        _lenS2 = 375 - jax.random.randint(jax.random.fold_in(_rk, 8), (32,), 0, max(1, 375 // 4) + 1, jnp.int32)
        _ctx_1024P = jax.random.normal(jax.random.fold_in(_rk, 11), (32, 16, 256), jnp.float32)
        _ctx_1024c = jax.random.dirichlet(jax.random.fold_in(_rk, 511), 0.3 * jnp.ones((16,), jnp.float32), (32, 375))
        _ctx_1024t = jnp.einsum('bsk,bkd->bsd', _ctx_1024c, _ctx_1024P)
        _ctx_1024t = _ctx_1024t * jax.lax.rsqrt(jnp.mean(jnp.square(_ctx_1024t)) + 1e-12) * 0.953939
        ctx_1024 = -0.000125008 + 0.999885 * (_ctx_1024t + 0.3 * jax.random.normal(jax.random.fold_in(_rk, 611), (32, 375, 256), jnp.float32))
        _g = jax.random.normal(jax.random.fold_in(_rk, 9001), (2, 1), jnp.float32)
        _g = jnp.sign(_g) * jnp.maximum(jnp.abs(_g), 1.0) + (_g == 0) * 1.0
        g_xattn = _g[0]
        g_ffn = _g[1]
        return (x, ctx_1024, g_xattn, g_ffn)
    x, ctx_1024, g_xattn, g_ffn = _rec_inputs()

    def _L0_xattn_setup():
        import jax, jax.numpy as jnp
        import numpy as np
        EPS = 1e-05

        def layer_norm(x, g, b):
            mu = jnp.mean(x, axis=-1, keepdims=True)
            var = jnp.var(x, axis=-1, keepdims=True)
            return (x - mu) * jax.lax.rsqrt(var + EPS) * g + b
        key = jax.random.key(seed)
        ks = jax.random.split(key, 8)
        dim, heads, dim_head = (256, 16, 64)
        inner = heads * dim_head
        b, n, m = (8, 1024, 64)
        s = dim ** (-0.5)
        return {'x': jax.random.normal(ks[0], (b, n, dim), jnp.float32), 'latents': jax.random.normal(ks[1], (b, m, dim), jnp.float32), 'ln_m_g': jnp.ones((dim,), jnp.float32), 'ln_m_b': jnp.zeros((dim,), jnp.float32), 'ln_l_g': jnp.ones((dim,), jnp.float32), 'ln_l_b': jnp.zeros((dim,), jnp.float32), 'Wq': jax.random.normal(ks[2], (dim, inner), jnp.float32) * s, 'Wkv': jax.random.normal(ks[3], (dim, 2 * inner), jnp.float32) * s, 'Wout': jax.random.normal(ks[4], (inner, dim), jnp.float32) * s}
    _L0_xattn_all = _L0_xattn_setup()
    _L0_xattn_in = {k: v for k, v in _L0_xattn_all.items() if k in ('ln_m_g', 'ln_m_b', 'ln_l_g', 'ln_l_b', 'Wq', 'Wkv', 'Wout')}
    del _L0_xattn_all

    def _L0_ffn_setup():
        import jax, jax.numpy as jnp
        import numpy as np
        TOP_K = 2
        key = jax.random.key(seed)
        ks = jax.random.split(key, 6)
        B, S, D, F, E = (2, 512, 256, 1024, 8)
        sd = 1.0 / np.sqrt(D)
        sf = 1.0 / np.sqrt(F)
        return {'x': jax.random.normal(ks[0], (B, S, D), jnp.float32), 'gate_w': jax.random.normal(ks[1], (D, E), jnp.float32) * sd, 'w1': jax.random.normal(ks[2], (E, D, F), jnp.float32) * sd, 'b1': jax.random.normal(ks[3], (E, F), jnp.float32) * 0.01, 'w2': jax.random.normal(ks[4], (E, F, D), jnp.float32) * sf, 'b2': jax.random.normal(ks[5], (E, D), jnp.float32) * 0.01}
    _L0_ffn_all = _L0_ffn_setup()
    _L0_ffn_in = {k: v for k, v in _L0_ffn_all.items() if k in ('gate_w', 'w1', 'b1', 'w2', 'b2')}
    del _L0_ffn_all
    return {'x': x, 'ctx_1024': ctx_1024, 'g_xattn': g_xattn, 'g_ffn': g_ffn, 'L0_xattn_ln_m_g': _L0_xattn_in['ln_m_g'], 'L0_xattn_ln_m_b': _L0_xattn_in['ln_m_b'], 'L0_xattn_ln_l_g': _L0_xattn_in['ln_l_g'], 'L0_xattn_ln_l_b': _L0_xattn_in['ln_l_b'], 'L0_xattn_Wq': _L0_xattn_in['Wq'], 'L0_xattn_Wkv': _L0_xattn_in['Wkv'], 'L0_xattn_Wout': _L0_xattn_in['Wout'], 'L0_ffn_gate_w': _L0_ffn_in['gate_w'], 'L0_ffn_w1': _L0_ffn_in['w1'], 'L0_ffn_b1': _L0_ffn_in['b1'], 'L0_ffn_w2': _L0_ffn_in['w2'], 'L0_ffn_b2': _L0_ffn_in['b2']}

def reference(x, ctx_1024, g_xattn, g_ffn, L0_xattn_ln_m_g, L0_xattn_ln_m_b, L0_xattn_ln_l_g, L0_xattn_ln_l_b, L0_xattn_Wq, L0_xattn_Wkv, L0_xattn_Wout, L0_ffn_gate_w, L0_ffn_w1, L0_ffn_b1, L0_ffn_w2, L0_ffn_b2):
    import jax
    import jax.numpy as jnp

    def _L0_xattn_ref(x, latents, ln_m_g, ln_m_b, ln_l_g, ln_l_b, Wq, Wkv, Wout):
        import jax, jax.numpy as jnp
        import numpy as np
        EPS = 1e-05

        def layer_norm(x, g, b):
            mu = jnp.mean(x, axis=-1, keepdims=True)
            var = jnp.var(x, axis=-1, keepdims=True)
            return (x - mu) * jax.lax.rsqrt(var + EPS) * g + b
        heads, dim_head = (16, 64)
        scale = dim_head ** (-0.5)
        x = layer_norm(x, ln_m_g, ln_m_b)
        lat = layer_norm(latents, ln_l_g, ln_l_b)
        b, m, _ = lat.shape
        q = lat @ Wq
        kv_input = jnp.concatenate([x, lat], axis=1)
        kv = kv_input @ Wkv
        k, v = jnp.split(kv, 2, axis=-1)

        def split_heads(t):
            return t.reshape(t.shape[0], t.shape[1], heads, dim_head).transpose(0, 2, 1, 3)
        q, k, v = (split_heads(q), split_heads(k), split_heads(v))
        dots = jnp.einsum('bhid,bhjd->bhij', q, k) * scale
        attn = jax.nn.softmax(dots, axis=-1)
        out = jnp.einsum('bhij,bhjd->bhid', attn, v)
        out = out.transpose(0, 2, 1, 3).reshape(b, m, heads * dim_head)
        return out @ Wout

    def _L0_ffn_ref(x, gate_w, w1, b1, w2, b2):
        import jax, jax.numpy as jnp
        import numpy as np
        TOP_K = 2
        B, S, D = x.shape
        T = B * S
        xf = x.reshape(T, D)
        gate_scores = jax.nn.softmax(xf @ gate_w, axis=-1)
        topk_scores, topk_idx = jax.lax.top_k(gate_scores, TOP_K)
        topk_scores = topk_scores / jnp.sum(topk_scores, axis=-1, keepdims=True)
        h = jax.nn.gelu(jnp.einsum('td,edf->etf', xf, w1) + b1[:, None, :], approximate=False)
        y = jnp.einsum('etf,efd->etd', h, w2) + b2[:, None, :]
        tok = jnp.arange(T)
        y_sel = y[topk_idx.T, tok[None, :]]
        out = jnp.einsum('kt,ktd->td', topk_scores.T, y_sel)
        return out.reshape(B, S, D)
    x = x + jnp.tanh(g_xattn[0]) * _L0_xattn_ref(ctx_1024, _layernorm(x, axis=-1), L0_xattn_ln_m_g, L0_xattn_ln_m_b, L0_xattn_ln_l_g, L0_xattn_ln_l_b, L0_xattn_Wq, L0_xattn_Wkv, L0_xattn_Wout)
    x = x + jnp.tanh(g_ffn[0]) * _L0_ffn_ref(_layernorm(x, axis=-1), L0_ffn_gate_w, L0_ffn_w1, L0_ffn_b1, L0_ffn_w2, L0_ffn_b2)
    return x

_drawn_inputs = setup_inputs


def setup_inputs(seed=0):
    import zlib

    import numpy as np

    out = dict(_drawn_inputs(seed))
    spreads = {'L0_xattn_ln_m_g': (1.0, 0.2),
     'L0_xattn_ln_m_b': (0.0, 0.1),
     'L0_xattn_ln_l_g': (1.0, 0.2),
     'L0_xattn_ln_l_b': (0.0, 0.1)}
    factors = {'L0_ffn_b1': 8.0, 'L0_ffn_b2': 8.0}
    for name, (base, spread) in spreads.items():
        noise = np.random.default_rng([zlib.crc32(name.encode()), seed]).standard_normal(out[name].shape)
        drawn = base * np.exp(spread * noise) if base else spread * noise
        out[name] = jnp.asarray(drawn.astype(out[name].dtype))
    for name, factor in factors.items():
        out[name] = (out[name] * factor).astype(out[name].dtype)
    return out
```

```python
import concourse.bass as bass
from concourse import mybir
from contextlib import ExitStack

F32 = mybir.dt.float32
F32R = mybir.dt.float32r
I32 = mybir.dt.int32
U32 = mybir.dt.uint32
ALU = mybir.AluOpType
ACT = mybir.ActivationFunctionType
AX = mybir.AxisListType

NB, LQ, LC, D = 32, 112, 375, 256
H, DH = 16, 64
LK = LC + LQ
LKP = LK + LK % 2
KD = D // 128
CT, CP = 3, LC // 3
NP = H // 2
KT = 4
INNER = H * DH
E, TOPK, F = 8, 2, 1024
EPS = 1e-5
TILES = (NB * LQ * TOPK + E * 127) // 128
UNITS = 20


class Batch:

    def __init__(self, at, i=None, step=0):
        self.at, self.i, self.step = at, i, step

    def __call__(self, per, extra=0):
        fixed = self.at * per + extra
        return fixed if self.i is None else self.i * (self.step * per) + fixed

    def has(self, offset):
        return self.i is not None or 0 <= self.at + offset < NB

    def halves(self, offset, per):
        fixed = per * ((self.at + offset) // 2 + 1)
        return fixed if self.i is None else self.i * (self.step // 2 * per) + fixed

    def parity(self, offset):
        return (self.at + offset) % 2


def batches(engine, body):
    for b in range(-2, 3):
        body(Batch(b))
    with engine.Fori(0, (NB - 6) // 2) as i:
        body(Batch(3, i, 2))
        body(Batch(4, i, 2))
    for b in range(NB - 3, NB + 1):
        body(Batch(b))


def units_of(b):
    if b.i is None and not -2 <= b.at <= NB:
        return []
    found = []
    kq, v = 0, 0
    for j in range(NP):
        if b.has(1):
            found.append(("K", j, b(10, 10 + kq + 1)))
            kq += 1
            found.append(("V", j, b(8, 8 + v + 1)))
            v += 1
        if b.has(2) and j in (4, 5):
            found.append(("T", j - 4, b(2, 4 + j - 4 + 1)))
        if b.has(1) and j in (6, 7):
            found.append(("Q", j - 6, b(10, 10 + kq + 1)))
            kq += 1
    return found


def first_unit(b):
    if b.i is None and b.at == -2:
        return 0
    return b(UNITS, 2 + UNITS)


def before(b):
    return Batch(b.at - 1, b.i, b.step)


def lag_batch(b):
    return b.i is not None or b.at >= 1


def prev_pair(b, j):
    return b.has(0) if j >= 1 else lag_batch(b)


def pv_pair(b, j):
    return b.has(0) if j >= 2 else lag_batch(b)


def attention(nc, x, ctx_in, g_x, ln_m_g, ln_m_b, ln_l_g, ln_l_b, wq, wkv, wout, gate_w, x2_out, xn_out, top_v, top_i, ident, sorted_x):
    with ExitStack() as st:
        sb = lambda name, shape, dt=F32: st.enter_context(nc.sbuf_tensor(name, shape, dt))
        sem = lambda name: st.enter_context(nc.semaphore(name))
        bank = lambda name: st.enter_context(nc.psum_tensor(name, [128, 512], F32))

        wkv_hi = sb("wkv_hi", [128, KD, 2 * INNER], F32R)
        wkv_lo = sb("wkv_lo", [128, KD, 2 * INNER], F32R)
        wq_sb = sb("wq_sb", [128, KD, INNER])
        wout_sb = sb("wout_sb", [128, NP, D])
        gate_sb = sb("gate_sb", [128, KD, E])
        affine = sb("affine", [128, 4, KD])
        tanh_g = sb("tanh_g", [128, 1])
        ctx_sb = sb("ctx_sb", [128, 2, CT, D])
        x_sb = sb("x_sb", [128, 2, D])
        norm_sb = sb("norm_sb", [128, CT + 1, D])
        stats = sb("stats", [128, CT + 1, 6])
        moments = sb("moments", [128, CT + 1, 2])
        rstd = sb("rstd", [128, 4 * (CT + 1)])
        half = sb("half", [128, CT + 1])
        eps = sb("eps", [128, CT + 1])
        kv_f = sb("kv_f", [128, KD, LKP])
        lat_f = sb("lat_f", [128, 2, KD, LQ])
        kv_hi = sb("kv_hi", [128, 2, KD, LKP], F32R)
        kv_lo = sb("kv_lo", [128, 2, KD, LKP], F32R)
        q_hi = sb("q_hi", [128, 2, NP, LQ], F32R)
        q_lo = sb("q_lo", [128, 2, NP, LQ], F32R)
        k_hi = sb("k_hi", [128, NP, LKP], F32R)
        k_lo = sb("k_lo", [128, NP, LKP], F32R)
        v_sb = sb("v_sb", [128, 2, KT, INNER])
        p_sb = sb("p_sb", [128, 2, 2, 512])
        pt_sb = sb("pt_sb", [128, 2, 2, KT, LQ])
        neg_max = sb("neg_max", [128, 2, 2])
        row_sum = sb("row_sum", [128, 2, 2])
        inv_sum = sb("inv_sum", [128, 2, 2])
        o_sb = sb("o_sb", [128, 2, NP, LQ])
        res_sb = sb("res_sb", [128, 2, D])
        x2_sb = sb("x2_sb", [128, 2, D])
        xn_sb = sb("xn_sb", [128, 2, D])
        stats2 = sb("stats2", [128, 6])
        moments2 = sb("moments2", [128, 2])
        rstd2 = sb("rstd2", [128, 2])
        xnt_sb = sb("xnt_sb", [128, KD, LQ])
        logits_sb = sb("logits_sb", [128, E])
        max_v = sb("max_v", [128, 8])
        max_i = sb("max_i", [128, 8], U32)
        zero_sb = sb("zero_sb", [128, D])

        scores_ps = [bank("scores_ps0"), bank("scores_ps1")]
        pt_ps = [bank("pt_ps0"), bank("pt_ps1")]
        proj_ps = [bank("proj_ps0"), bank("proj_ps1")]
        pv_ps = bank("pv_ps")
        tail_ps = bank("tail_ps")

        w_loaded = sem("w_loaded"); small_loaded = sem("small_loaded")
        zeroed = sem("zeroed")
        w_hi_done = sem("w_hi_done"); w_ready = sem("w_ready"); set_up = sem("set_up"); tanh_done = sem("tanh_done")
        ctx_loaded = [sem("ctx_loaded0"), sem("ctx_loaded1")]
        res_loaded = [sem("res_loaded0"), sem("res_loaded1")]
        stats_done = sem("stats_done"); moments_done = sem("moments_done"); rstd_done = sem("rstd_done"); pool_step = sem("pool_step")
        norm_done = sem("norm_done")
        proj_done = sem("proj_done"); kq_hi = sem("kq_hi"); kq_lo = sem("kq_lo"); v_copied = sem("v_copied")
        kv_affine = sem("kv_affine"); kvhi_done = sem("kvhi_done"); kvlo_done = sem("kvlo_done")
        scores_done = sem("scores_done"); max_done = sem("max_done"); exp_done = sem("exp_done"); inv_done = sem("inv_done"); p_ready = sem("p_ready")
        pt_done = sem("pt_done"); pt_copied = [sem("pt_copied_act"), sem("pt_copied_dve")]
        pv_done = sem("pv_done"); o_copied = sem("o_copied")
        out_done = sem("out_done"); x2_done = sem("x2_done"); stats2_done = sem("stats2_done"); rstd2_done = sem("rstd2_done")
        xn_done = sem("xn_done"); xnt_done = sem("xnt_done"); xnt_copied = sem("xnt_copied"); logits_done = sem("logits_done")
        logits_copied = sem("logits_copied"); top_done = sem("top_done"); stored = [sem("stored0"), sem("stored1")]

        block = st.enter_context(nc.Block())

        stage = v_sb[:, :, :, :].rearrange("p a b c -> p (a b c)")[:, 0:KD * 2 * INNER].rearrange("p (k n) -> p k n", k=KD)

        @block.sync
        def _(sp):
            sp.dma_start(stage, wkv.rearrange("(k p) n -> p k n", p=128)).then_inc(w_loaded, 16)
            for n, a in enumerate((ln_m_g, ln_m_b, ln_l_g, ln_l_b)):
                sp.dma_start(affine[:, n, :], a.rearrange("(k p) -> p k", p=128), allow_slow_non_contiguous=True).then_inc(small_loaded, 16)
            sp.dma_start(tanh_g[:, :], g_x.partition_broadcast(128)).then_inc(small_loaded, 16)
            sp.dma_start(gate_sb[:, :, :], gate_w.rearrange("(k p) e -> p k e", p=128)).then_inc(small_loaded, 16)

            def load(b, off):
                s = b.parity(off)
                c = b(1, off)
                cx = ctx_in[c] if isinstance(c, int) else ctx_in[bass.ds(c, 1)].rearrange("o n d -> (o n) d")
                xx = x[c] if isinstance(c, int) else x[bass.ds(c, 1)].rearrange("o n d -> (o n) d")
                sp.dma_start(ctx_sb[0:CP, s], cx.rearrange("(t p) d -> p t d", p=CP)).then_inc(ctx_loaded[s], 16)
                sp.dma_start(x_sb[0:LQ, s], xx).then_inc(ctx_loaded[s], 16)

            load(Batch(0), 0)
            load(Batch(0), 1)
            sp.dma_start(wq_sb[:, :, :], wq.rearrange("(k p) n -> p k n", p=128)).then_inc(small_loaded, 16)
            sp.dma_start(wout_sb[:, :, :], wout.rearrange("(j p) n -> p j n", p=128)).then_inc(small_loaded, 16)

            def body(b):
                if b.has(3) and not (b.i is None and b.at < -1):
                    sp.wait_ge(norm_done, b(1, 2))
                    load(b, 3)
                if b.has(0):
                    s = b.parity(0)
                    if b.at >= 2:
                        sp.wait_ge(x2_done, b(1, -1))
                    c = b(1)
                    xx = x[c] if isinstance(c, int) else x[bass.ds(c, 1)].rearrange("o n d -> (o n) d")
                    sp.dma_start(res_sb[0:LQ, s], xx).then_inc(res_loaded[s], 16)
                if b.has(-1) and not (b.i is None and b.at < 1):
                    s = b.parity(-1)
                    c = b(1, -1)
                    o1, o2 = (t[c] if isinstance(c, int) else t[bass.ds(c, 1)].rearrange("o n d -> (o n) d") for t in (x2_out, xn_out))
                    sp.wait_ge(x2_done, b(1))
                    sp.dma_start(o1, x2_sb[0:LQ, s]).then_inc(stored[s], 16)
                    sp.wait_ge(xn_done, b(1))
                    sp.dma_start(o2, xn_sb[0:LQ, s]).then_inc(stored[s], 16)

            batches(sp, body)
            for s in stored:
                sp.wait_ge(s, NB // 2 * 32)

        @block.gpsimd
        def _(pool):
            pool.memset(ident[:, :], 0.0).then_inc(pool_step, 1)
            pool.memset(half[:, :], -0.5).then_inc(pool_step, 1)
            pool.wait_ge(pool_step, 2)
            pool.affine_select(out=ident[:, :], in_=ident[:, :], compare_op=ALU.not_equal, fill=1.0, base=0,
                               pattern=[[-1, 128]], channel_multiplier=1).then_inc(pool_step, 1)
            pool.memset(kv_f[:, :, LK:LKP], 0.0).then_inc(pool_step, 1)
            for s in range(2):
                for h in range(2):
                    pool.memset(p_sb[0:LQ, s, h, LK:512], 0.0).then_inc(pool_step, 1)
            pool.memset(moments[:, :, :], 1.0).then_inc(pool_step, 1)
            pool.memset(zero_sb[:, :], 0.0).then_inc(pool_step, 1)
            pool.memset(eps[:, :], EPS).then_inc(pool_step, 1)
            pool.wait_ge(pool_step, 11)
            pool.sem_inc(set_up, 1)
            slots = sorted_x.rearrange("(t p) d -> t p d", p=128)
            for t in range(TILES):
                pool.dma_start(slots[t], zero_sb[:, :]).then_inc(zeroed, 16)
            pool.wait_ge(zeroed, 16 * TILES)

            N = CT + 1
            r = lambda a, k=None: rstd[0:CP, a * N:(a + 1) * N] if k is None else rstd[0:LQ, a * N + CT:a * N + CT + 1]
            COUNT = 6

            def body(b):
                if b.has(2):
                    base = b(COUNT, 2 * COUNT + 11)
                    s = b.parity(2)
                    v = moments[0:CP, :, 1]
                    pool.wait_ge(moments_done, b(1, 3))
                    if b.i is not None or b.at > -2:
                        pool.wait_ge(norm_done, b(1, 2))
                    pool.tensor_tensor(r(0), v, eps[0:CP, :], ALU.add).then_inc(pool_step, 1)
                    pool.wait_ge(pool_step, b(COUNT, 2 * COUNT + 11 + 1))
                    pool.tensor_tensor(r(1), r(0), half[0:CP, :], ALU.pow).then_inc(pool_step, 1)
                    pool.wait_ge(pool_step, b(COUNT, 2 * COUNT + 11 + 2))
                    lv = moments[0:LQ, CT:CT + 1, 1]
                    pool.tensor_tensor(r(2, 1), r(1, 1), r(1, 1), ALU.mult).then_inc(pool_step, 1)
                    pool.wait_ge(pool_step, b(COUNT, 2 * COUNT + 11 + 3))
                    pool.tensor_tensor(r(3, 1), r(2, 1), lv, ALU.mult).then_inc(pool_step, 1)
                    pool.wait_ge(pool_step, b(COUNT, 2 * COUNT + 11 + 4))
                    pool.tensor_tensor(r(2, 1), r(3, 1), eps[0:LQ, 0:1], ALU.add).then_inc(pool_step, 1)
                    pool.wait_ge(pool_step, b(COUNT, 2 * COUNT + 11 + 5))
                    pool.tensor_tensor(r(3, 1), r(2, 1), half[0:LQ, 0:1], ALU.pow).then_inc(pool_step, 1)
                    pool.wait_ge(pool_step, b(COUNT, 2 * COUNT + 11 + 6))
                    pool.tensor_tensor(r(1, 1), r(1, 1), r(3, 1), ALU.mult).then_inc(rstd_done, 1)
                if b.has(-1) and not (b.i is None and b.at < 1):
                    pool.wait_ge(stats2_done, b(2))
                    pool.tensor_tensor(rstd2[0:LQ, 0:1], moments2[0:LQ, 1:2], eps[0:LQ, 0:1], ALU.add).then_inc(rstd2_done, 1)
                    pool.wait_ge(rstd2_done, b(2, -1))
                    pool.tensor_tensor(rstd2[0:LQ, 1:2], rstd2[0:LQ, 0:1], half[0:LQ, 0:1], ALU.pow).then_inc(rstd2_done, 1)
                if b.has(2):
                    for k in range(KD):
                        pool.wait_ge(kvhi_done, b(2, 4 + k + 1))
                        pool.tensor_tensor(kv_lo[:, s, k], kv_f[:, k], kv_hi[:, s, k].bitcast(F32), ALU.subtract).then_inc(kvlo_done, 1)

            batches(pool, body)

        @block.scalar
        def _(act):
            act.wait_ge(small_loaded, 16 * 8)
            act.activation(tanh_g[:, :], tanh_g[:, :], ACT.Tanh).then_inc(tanh_done, 1)

            def body(b):
                n = first_unit(b)
                units = units_of(b)
                kq = v = 0

                def kq_high(kind, j, k):
                    act.wait_ge(proj_done, unit_end)
                    if kind == "K":
                        act.activation(k_hi[:, j], proj_ps[k][:, 0:LKP], ACT.Copy).then_inc(kq_hi, 1)
                    else:
                        s = b.parity(1)
                        act.activation(q_hi[:, s, j * 4:j * 4 + 4], proj_ps[k][:, 0:4 * LQ].rearrange("p (j q) -> p j q", j=4),
                                       ACT.Copy, scale=float(DH) ** -0.5).then_inc(kq_hi, 1)

                count = 0
                for j in range(NP):
                    if b.has(0):
                        for h in range(2):
                            act.wait_ge(max_done, b(H, 2 * j + h + 1))
                            act.activation(p_sb[0:LQ, j % 2, h, 0:LK], scores_ps[h][0:LQ, 0:LK], ACT.Exp,
                                           bias=neg_max[0:LQ, j % 2, h:h + 1], accum_out=row_sum[0:LQ, j % 2, h:h + 1]).then_inc(exp_done, 1)
                    if b.has(1):
                        unit_end = first_unit(b) + count + 1
                        kq_high("K", j, count % 2)
                        count += 1
                    if prev_pair(b, j):
                        act.wait_ge(pt_done, b(H, 2 * j - 1))
                        act.activation(pt_sb[:, (j - 1) % 2, 0], pt_ps[0][:, 0:KT * LQ].rearrange("p (t q) -> p t q", t=KT), ACT.Copy).then_inc(pt_copied[0], 1)
                    if b.has(1):
                        act.wait_ge(proj_done, first_unit(b) + count + 1)
                        t, half_ = j % KT, j // KT
                        rows = 128 if t < KT - 1 else LKP - 128 * (KT - 1)
                        if b.i is None and b.at == -1 and j == 0:
                            act.wait_ge(w_ready, 2)
                        act.activation(v_sb[0:rows, b.parity(1), t, half_ * 512:half_ * 512 + 512], proj_ps[count % 2][0:rows, :], ACT.Copy).then_inc(v_copied, 1)
                        count += 1
                    if b.has(2) and j in (4, 5):
                        k = j - 4
                        act.wait_ge(kv_affine, b(2, 4 + k + 1))
                        act.activation(kv_hi[:, b.parity(2), k], kv_f[:, k], ACT.Copy).then_inc(kvhi_done, 1)
                        count += 1
                    if b.has(1) and j in (6, 7):
                        unit_end = first_unit(b) + count + 1
                        kq_high("Q", j - 6, count % 2)
                        count += 1
                    if lag_batch(b) and j == 5:
                        act.wait_ge(xnt_done, b(1))
                        act.activation(xnt_sb[:, :, :], tail_ps[:, 0:KD * LQ].rearrange("p (k q) -> p k q", k=KD), ACT.Copy).then_inc(xnt_copied, 1)

            batches(act, body)

        @block.vector
        def _(dve):
            dve.wait_ge(w_loaded, 16)
            for k in range(KD):
                dve.tensor_copy(wkv_hi[:, k], stage[:, k]).then_inc(w_hi_done, 1)
            for k in range(KD):
                dve.wait_ge(w_hi_done, k + 1)
                dve.tensor_tensor(wkv_lo[:, k], stage[:, k], wkv_hi[:, k].bitcast(F32), ALU.subtract).then_inc(w_hi_done, 1)
            dve.wait_ge(w_hi_done, 4)
            for s in range(2):
                dve.memset(v_sb[96:128, s, KT - 1], 0.0).then_inc(w_ready, 1)
            dve.wait_ge(set_up, 1)
            dve.wait_ge(small_loaded, 16 * 8)
            dve.wait_ge(tanh_done, 1)

            def body(b):
                base = first_unit(b)
                count = 0

                def low(kind, j, slot):
                    dve.wait_ge(kq_hi, idx)
                    if kind == "K":
                        dve.tensor_tensor(k_lo[:, j], proj_ps[slot][:, 0:LKP], k_hi[:, j].bitcast(F32), ALU.subtract).then_inc(kq_lo, 1)
                    else:
                        s = b.parity(1)
                        v = lambda t: t[:, s, j * 4:j * 4 + 4].rearrange("p j q -> p (j q)")
                        dve.scalar_tensor_tensor(out=v(q_lo), in0=proj_ps[slot][:, 0:4 * LQ], scalar=float(DH) ** -0.5,
                                                 in1=v(q_hi).bitcast(F32), op0=ALU.mult, op1=ALU.subtract).then_inc(kq_lo, 1)

                kq = 0
                for j in range(NP):
                    if b.has(2) and j == 1:
                        dve.wait_ge(stats_done, b(CT + 1, 3 * (CT + 1)))
                    if lag_batch(b) and j == 3:
                        dve.wait_ge(stats2_done, b(2, -1))
                    if lag_batch(b) and j == 7:
                        dve.wait_ge(logits_copied, b(1))
                    if b.has(0):
                        for h in range(2):
                            dve.wait_ge(scores_done, b(H, 2 * j + h + 1))
                            dve.tensor_reduce(neg_max[0:LQ, j % 2, h:h + 1], scores_ps[h][0:LQ, 0:LK], AX.X, ALU.max, negate=True).then_inc(max_done, 1)
                    if lag_batch(b) and j == 7:
                        dve.max(max_v[0:LQ, :], logits_sb[0:LQ, :]).then_inc(top_done, 1)
                        dve.wait_ge(top_done, b(2, -1))
                    if b.has(1):
                        idx = b(10, 10 + kq + 1)
                        low("K", j, count % 2)
                        kq += 1
                        count += 2
                    if lag_batch(b) and j == 7:
                        dve.max_index(max_i[0:LQ, :], max_v[0:LQ, :], logits_sb[0:LQ, :]).then_inc(top_done, 1)
                        dve.wait_ge(top_done, b(2))
                    if prev_pair(b, j):
                        dve.wait_ge(pt_done, b(H, 2 * j))
                        dve.tensor_copy(pt_sb[:, (j - 1) % 2, 1], pt_ps[1][:, 0:KT * LQ].rearrange("p (t q) -> p t q", t=KT)).then_inc(pt_copied[1], 1)
                    if b.has(0):
                        for h in range(2):
                            dve.wait_ge(exp_done, b(H, 2 * j + h + 1))
                            dve.reciprocal(inv_sum[0:LQ, j % 2, h:h + 1], row_sum[0:LQ, j % 2, h:h + 1]).then_inc(inv_done, 1)
                        for h in range(2):
                            dve.wait_ge(inv_done, b(H, 2 * j + h + 1))
                            dve.tensor_scalar(p_sb[0:LQ, j % 2, h, 0:LK], p_sb[0:LQ, j % 2, h, 0:LK], inv_sum[0:LQ, j % 2, h:h + 1], None, ALU.mult).then_inc(p_ready, 1)
                    if pv_pair(b, j):
                        p = (j - 2) % NP
                        so = b.parity(0 if j >= 2 else -1)
                        dve.wait_ge(pv_done, b(NP, j - 1))
                        dve.tensor_copy(o_sb[:, so, p], pv_ps[:, 0:LQ]).then_inc(o_copied, 1)
                    if b.has(2) and j == 0:
                        s = b.parity(2)
                        dve.wait_ge(ctx_loaded[s], b.halves(2, 32))
                        if b.i is not None or b.at > -2:
                            dve.wait_ge(rstd_done, b(1, 2))
                            dve.wait_ge(norm_done, b(1, 2))
                        for t in range(CT + 1):
                            rows = ctx_sb[0:CP, s, t] if t < CT else x_sb[0:LQ, s]
                            dve.bn_stats(stats[0:rows.shape[0], t], rows).then_inc(stats_done, 1)
                    if b.has(2) and j == 1:
                        for t in range(CT + 1):
                            n = CP if t < CT else LQ
                            last = dve.bn_aggr(moments[0:n, t], stats[0:n, t])
                        last.then_inc(moments_done, 1)
                    if b.has(2) and j == 2:
                        dve.wait_ge(rstd_done, b(1, 3))
                        for t in range(CT + 1):
                            n = CP if t < CT else LQ
                            rows = ctx_sb[0:CP, s, t] if t < CT else x_sb[0:LQ, s]
                            last = dve.tensor_scalar(norm_sb[0:n, t], rows, moments[0:n, t, 0:1], rstd[0:n, CT + 1 + t:CT + 2 + t], ALU.subtract, ALU.mult)
                        last.then_inc(norm_done, 1)
                    if b.has(2) and j in (4, 5):
                        k = j - 4
                        dve.wait_ge(proj_done, base + count + 1)
                        if b.i is not None or b.at > -2:
                            dve.wait_ge(kvlo_done, b(2, 2 + k + 1))
                        dve.tensor_scalar(kv_f[:, k, 0:LC], proj_ps[count % 2][:, 0:LC], affine[:, 0, k:k + 1], affine[:, 1, k:k + 1], ALU.mult, ALU.add)
                        dve.tensor_scalar(kv_f[:, k, LC:LK], proj_ps[count % 2][:, LC:LK], affine[:, 2, k:k + 1], affine[:, 3, k:k + 1], ALU.mult, ALU.add)
                        dve.tensor_scalar(lat_f[:, s, k], proj_ps[count % 2][:, LC:LK], affine[:, 2, k:k + 1], affine[:, 3, k:k + 1], ALU.mult, ALU.add).then_inc(kv_affine, 1)
                        count += 1
                    if b.has(1) and j in (6, 7):
                        idx = b(10, 10 + kq + 1)
                        low("Q", j - 6, count % 2)
                        kq += 1
                        count += 1
                    if lag_batch(b):
                        sl = b.parity(-1)
                        if j == 2:
                            dve.wait_ge(out_done, b(1))
                            dve.wait_ge(res_loaded[sl], b.halves(-1, 16))
                            if b.i is not None or b.at >= 3:
                                dve.wait_ge(stored[sl], b.halves(-3, 32))
                            dve.scalar_tensor_tensor(out=x2_sb[0:LQ, sl], in0=tail_ps[0:LQ, 0:D], scalar=tanh_g[0:LQ, 0:1], in1=res_sb[0:LQ, sl],
                                                     op0=ALU.mult, op1=ALU.add).then_inc(x2_done, 1)
                            dve.wait_ge(x2_done, b(1))
                            dve.bn_stats(stats2[0:LQ, :], x2_sb[0:LQ, sl]).then_inc(stats2_done, 1)
                        if j == 3:
                            dve.bn_aggr(moments2[0:LQ, :], stats2[0:LQ, :]).then_inc(stats2_done, 1)
                        if j == 4:
                            dve.wait_ge(rstd2_done, b(2))
                            dve.tensor_scalar(xn_sb[0:LQ, sl], x2_sb[0:LQ, sl], moments2[0:LQ, 0:1], rstd2[0:LQ, 1:2], ALU.subtract, ALU.mult).then_inc(xn_done, 1)
                        if j == 6:
                            dve.wait_ge(logits_done, b(1))
                            dve.tensor_copy(logits_sb[0:LQ, :], tail_ps[0:LQ, 256:256 + E]).then_inc(logits_copied, 1)
                        if j == 7:
                            c = b(1, -1)
                            to = lambda t: t[0:LQ, c] if isinstance(c, int) else t[0:LQ, bass.ds(c, 1)].rearrange("p o k -> p (o k)")
                            dve.tensor_copy(to(top_v), max_v[0:LQ, 0:TOPK])
                            dve.tensor_copy(to(top_i), max_i[0:LQ, 0:TOPK])

            batches(dve, body)

        @block.tensor
        def _(pe):
            pe.wait_ge(set_up, 1)

            def free(kind, idx):
                sem_ = {"K": kq_lo, "Q": kq_lo, "V": v_copied, "T": kv_affine}[kind]
                pe.wait_ge(sem_, idx)

            def body(b):
                units = units_of(b)
                earlier = units_of(before(b))[-2:]
                seq = earlier + units
                pos = [0]

                def take():
                    i = pos[0]
                    pos[0] += 1
                    back = i + len(earlier) - 2
                    if back >= 0:
                        free(seq[back][0], seq[back][2])
                    return proj_ps[i % 2]

                def three(out, lhs, rhs):
                    n = 0
                    for k in range(KD):
                        for a, c in ((0, 0), (0, 1), (1, 0)):
                            last = nc.tensor.matmul(out, lhs(a, k), rhs(c, k), start=(n == 0), stop=(n == 3 * KD - 1))
                            n += 1
                    return last

                for j in range(NP):
                    if b.has(0):
                        s = b.parity(0)
                        if j == 0:
                            pe.wait_ge(kq_lo, b(10, 10))
                        for h in range(2):
                            if j or lag_batch(b):
                                pe.wait_ge(exp_done, b(H, 2 * j + h - 1))
                            rows = slice(64 * h, 64 * h + 64)
                            for n, (qq, kk) in enumerate(((q_hi, k_hi), (q_hi, k_lo), (q_lo, k_hi))):
                                last = nc.tensor.matmul(scores_ps[h][0:LQ, 0:LKP], qq[rows, s, j], kk[rows, j], start=(n == 0), stop=(n == 2))
                            last.then_inc(scores_done, 1)
                    if b.has(1):
                        s1 = b.parity(1)
                        if j == 0:
                            pe.wait_ge(kvlo_done, b(2, 4))
                            if b.i is None and b.at == -1:
                                pe.wait_ge(w_ready, 2)
                        ps = take()
                        three(ps[:, 0:LKP], lambda a, k: (wkv_hi, wkv_lo)[a][:, k, j * 128:j * 128 + 128],
                              lambda c, k: (kv_hi, kv_lo)[c][:, s1, k]).then_inc(proj_done, 1)
                    if prev_pair(b, j):
                        for h in range(2):
                            pe.wait_ge(p_ready, b(H, 2 * j - 1 + h))
                            if j >= 2 or lag_batch(b):
                                pe.wait_ge(pt_copied[h], b(NP, j - 1))
                            for t in range(KT):
                                last = nc.tensor.transpose(pt_ps[h][:, t * LQ:(t + 1) * LQ], p_sb[0:LQ, (j - 1) % 2, h, t * 128:(t + 1) * 128], ident[0:LQ, 0:LQ])
                            last.then_inc(pt_done, 1)
                    if b.has(1):
                        t, half_ = j % KT, j // KT
                        rows = 128 if t < KT - 1 else LKP - 128 * (KT - 1)
                        ps = take()
                        three(ps[0:rows, :], lambda a, k: (kv_hi, kv_lo)[a][:, s1, k, t * 128:t * 128 + rows],
                              lambda c, k: (wkv_hi, wkv_lo)[c][:, k, INNER + half_ * 512:INNER + half_ * 512 + 512]).then_inc(proj_done, 1)
                    if pv_pair(b, j):
                        p = (j - 2) % NP
                        sv = b.parity(0 if j >= 2 else -1)
                        for h in range(2):
                            pe.wait_ge(pt_copied[h], b(NP, j - 1))
                        if j == 2:
                            pe.wait_ge(v_copied, b(8, 8))
                        if j >= 3 or lag_batch(b):
                            pe.wait_ge(o_copied, b(NP, j - 2))
                        for t in range(KT):
                            for h in range(2):
                                n = 2 * p + h
                                last = nc.tensor.matmul(pv_ps[64 * h:64 * h + 64, 0:LQ], v_sb[:, sv, t, n * DH:(n + 1) * DH], pt_sb[:, (j - 2) % 2, h, t],
                                                        start=(t == 0), stop=(t == KT - 1))
                        last.then_inc(pv_done, 1)
                    if lag_batch(b):
                        sl = b.parity(-1)
                        if j == 2:
                            pe.wait_ge(o_copied, b(NP))
                            if b.i is not None or b.at >= 2:
                                pe.wait_ge(logits_copied, b(1, -1))
                            for p in range(NP):
                                last = nc.tensor.matmul(tail_ps[0:LQ, 0:D], o_sb[:, sl, p], wout_sb[:, p], start=(p == 0), stop=(p == NP - 1))
                            last.then_inc(out_done, 1)
                        if j == 5:
                            pe.wait_ge(xn_done, b(1))
                            for k in range(KD):
                                last = nc.tensor.transpose(tail_ps[:, k * LQ:(k + 1) * LQ], xn_sb[0:LQ, sl, k * 128:(k + 1) * 128], ident[0:LQ, 0:LQ])
                            last.then_inc(xnt_done, 1)
                        if j == 6:
                            pe.wait_ge(xnt_copied, b(1))
                            for k in range(KD):
                                last = nc.tensor.matmul(tail_ps[0:LQ, 256:256 + E], xnt_sb[:, k], gate_sb[:, k], start=(k == 0), stop=(k == KD - 1))
                            last.then_inc(logits_done, 1)
                    if b.has(2) and j in (4, 5):
                        k = j - 4
                        if k == 0:
                            pe.wait_ge(norm_done, b(1, 3))
                        ps = take()
                        for t in range(CT):
                            nc.tensor.transpose(ps[:, t * CP:(t + 1) * CP], norm_sb[0:CP, t, k * 128:(k + 1) * 128], ident[0:CP, 0:CP])
                        nc.tensor.transpose(ps[:, LC:LK], norm_sb[0:LQ, CT, k * 128:(k + 1) * 128], ident[0:LQ, 0:LQ]).then_inc(proj_done, 1)
                    if b.has(1) and j in (6, 7):
                        ps = take()
                        for m in range(4):
                            jj = (j - 6) * 4 + m
                            for k in range(KD):
                                last = nc.tensor.matmul(ps[:, m * LQ:(m + 1) * LQ], wq_sb[:, k, jj * 128:jj * 128 + 128], lat_f[:, s1, k], start=(k == 0), stop=(k == KD - 1))
                        last.then_inc(proj_done, 1)

            batches(pe, body)

def routed_ffn(nc, g_x, w1, b1, w2, b2, x2_in, xn_in, out, sorted_x, sorted_y, top_v, top_i):
    NTOK = NB * TOPK
    with ExitStack() as st:
        sb = lambda name, shape, dt=F32: st.enter_context(nc.sbuf_tensor(name, shape, dt))
        sem = lambda name: st.enter_context(nc.semaphore(name))
        bank = lambda name: st.enter_context(nc.psum_tensor(name, [128, 512], F32))
        KF = F // 128

        w1_sb = sb("w1_sb", [128, KD, E, F])
        w2_sb = sb("w2_sb", [128, KF, E, D])
        b1_sb = sb("b1_sb", [128, E, F])
        xn_all = b1_sb[:, :, :].rearrange("p e f -> p (e f)").rearrange("p (b d) -> p b d", b=NB)
        b2_sb = sb("b2_sb", [128, E, D])
        x_sb = sb("xs_sb", [128, 2, D])
        xt_sb = sb("xt_sb", [128, 2, KD, 128])
        h_sb = sb("h_sb", [128, 2, 512])
        g_sb = sb("g_sb", [128, 2, 512])
        ht_sb = sb("ht_sb", [128, KF, 128])
        y_sb = sb("y_sb", [128, 2, D])
        ident2 = sb("ident2", [128, 128])

        onehot = sb("onehot", [128, E, TOPK, NB])
        member = sb("member", [128, E, NB])
        total = sb("total", [128, E, NB])
        slot = sb("slot", [128, E, NB])
        picked = sb("picked", [128, TOPK, E, NB])
        slot_f = sb("slot_f", [128, TOPK, NB])
        slot_i = sb("slot_i", [128, TOPK, NB], I32)
        top_f = sb("top_f", [128, TOPK, NB])
        count_f = sb("count_f", [128, E])
        count_i = sb("count_i", [128, 2, E], I32)
        tiles_f = sb("tiles_f", [128, E])
        tile_end = sb("tile_end", [128, E])
        slot_start = sb("slot_start", [128, E])
        ones = sb("ones", [128, 128])
        before_me = sb("before_me", [128, 128])
        tile_no = sb("tile_no", [1, TILES])
        tile_acc = sb("tile_acc", [1, 2, TILES])
        tile_expert = sb("tile_expert", [1, TILES], I32)
        weight = sb("weight", [128, TOPK, NB])
        ratio = sb("ratio", [128, 3, NB])
        tanh_f = sb("tanh_f", [128, 1])
        NG = E
        y_in = w1_sb[:, 0, :, 0:TOPK * D].rearrange("p s (k d) -> p s k d", k=TOPK)
        x2_sb, part_sb, o_sb = (w1_sb[:, 1, :, n * D:n * D + D] for n in range(3))

        h_ps = [bank("h_ps0"), bank("h_ps1")]
        ht_ps = [bank("ht_ps0"), bank("ht_ps1")]
        xt_ps = bank("xt_ps")
        y_ps = bank("y_ps")
        count_ps = bank("count_ps")

        made = sem("made"); xn_loaded = sem("xn_loaded"); weights_loaded = sem("weights_loaded"); tanh_loaded = sem("tanh_loaded")
        step = sem("step"); counted = sem("counted"); ratio_ready = sem("ratio_ready"); act_done = sem("act_done")
        slots_ready = sem("slots_ready"); scattered = sem("scattered"); scattered1 = sem("scattered1")
        x_loaded = [sem("xs_loaded0"), sem("xs_loaded1")]
        xt_done = sem("xt_done"); xt_copied = sem("xt_copied"); h_done = sem("h_done"); biased = sem("biased"); gelu_done = sem("gelu_done")
        ht_done = sem("ht_done"); ht_copied = [sem("ht_copied_act"), sem("ht_copied_dve")]
        y_done = sem("y_done"); y_ready = sem("y_ready"); y_stored = [sem("y_stored0"), sem("y_stored1")]
        gathered = [sem(f"gathered{i}") for i in range(NG)]
        x2_loaded = [sem(f"x2_loaded{i}") for i in range(NG)]
        part_done = sem("part_done"); out_ready = sem("out_ready"); out_stored = [sem(f"out_stored{i}") for i in range(NG)]

        block = st.enter_context(nc.Block())
        xs = sorted_x.rearrange("(t p) d -> t p d", p=128)
        ys = sorted_y.rearrange("(t p) d -> t p d", p=128)

        class Tile:
            def __init__(self, at, i=None):
                self.at, self.i = at, i

            def __call__(self, per, extra=0):
                fixed = self.at * per + extra
                return fixed if self.i is None else self.i * (2 * per) + fixed

            def halves(self, per, offset=0):
                fixed = per * ((self.at + offset) // 2 + 1)
                return fixed if self.i is None else self.i * per + fixed

            def has(self, offset):
                return self.i is not None or 0 <= self.at + offset < TILES

        def tiles(engine, body):
            for t in range(-2, 2):
                body(Tile(t))
            n = (TILES - 4) // 2
            with engine.Fori(0, n) as i:
                body(Tile(2, i))
                body(Tile(3, i))
            for t in range(2 + 2 * n, TILES):
                body(Tile(t))

        def row(tensor, c):
            return tensor[c] if isinstance(c, int) else tensor[bass.ds(c, 1)].rearrange("o p d -> (o p) d")

        @block.sync
        def _(sp):
            for n in range(4):
                sp.dma_start(xn_all[0:LQ, n * 8:n * 8 + 8], xn_in[n * 8:n * 8 + 8].rearrange("b p d -> p b d")).then_inc(xn_loaded, 16)
            sp.dma_start(tanh_f[:, :], g_x.partition_broadcast(128)).then_inc(tanh_loaded, 16)
            for e in range(E):
                sp.dma_start(w1_sb[:, :, e], w1[e].rearrange("(k p) f -> p k f", p=128)).then_inc(weights_loaded, 16)
                sp.dma_start(w2_sb[:, :, e], w2[e].rearrange("(k p) d -> p k d", p=128)).then_inc(weights_loaded, 16)
            sp.dma_start(b2_sb[:, :, :], b2.partition_broadcast(128)).then_inc(weights_loaded, 16)
            sp.wait_ge(scattered, 16 * NTOK)
            sp.dma_start(b1_sb[:, :, :], b1.partition_broadcast(128)).then_inc(weights_loaded, 16)

            def body(t):
                if t.has(2):
                    if t.at >= 0:
                        sp.wait_ge(xt_done, t(1, 1))
                    sp.dma_start(x_sb[:, t.at % 2], row(xs, t(1, 2))).then_inc(x_loaded[t.at % 2], 16)
                if t.has(0):
                    sp.wait_ge(y_ready, t(1, 1))
                    sp.dma_start(row(ys, t(1)), y_sb[:, t.at % 2]).then_inc(y_stored[t.at % 2], 16)

            tiles(sp, body)

            def store(b):
                sp.wait_ge(out_ready, b + 1)
                sp.dma_start(out[b], o_sb[0:LQ, b % NG]).then_inc(out_stored[b % NG], 16)

            sp.wait_ge(h_done, 2 * TILES)
            for b in range(NB):
                s = b % NG
                if b >= NG:
                    sp.wait_ge(part_done, b - NG + 1)
                sp.dma_start(x2_sb[0:LQ, s], x2_in[b]).then_inc(x2_loaded[s], 16)
                if b >= NG // 2:
                    store(b - NG // 2)
            for b in range(NB - NG // 2, NB):
                store(b)
            for s in range(NG):
                sp.wait_ge(out_stored[s], NB // NG * 16)

        @block.gpsimd
        def _(pool):
            pool.memset(ones[:, :], 1.0).then_inc(made, 1)
            pool.memset(ident2[:, :], 0.0).then_inc(made, 1)
            pool.wait_ge(made, 2)
            pool.affine_select(out=before_me[:, :], in_=ones[:, :], compare_op=ALU.is_gt, fill=0.0, base=0,
                               pattern=[[1, 128]], channel_multiplier=-1).then_inc(made, 1)
            pool.affine_select(out=ident2[:, :], in_=ident2[:, :], compare_op=ALU.not_equal, fill=1.0, base=0,
                               pattern=[[-1, 128]], channel_multiplier=1).then_inc(made, 1)
            pool.iota(tile_no[:, :], pattern=[[1, TILES]], base=0, channel_multiplier=0,
                      allow_small_or_imprecise_dtypes=True).then_inc(made, 1)
            pool.wait_ge(slots_ready, 1)
            pool.wait_ge(xn_loaded, 64)
            for b in range(NB):
                for k in range(TOPK):
                    pool.indirect_dma_start(sorted_x, bass.IndirectOffsetOnAxis(ap=slot_i[0:LQ, k, b:b + 1], axis=0), xn_all[0:LQ, b], None).then_inc(scattered, 16)
            for s in range(2):
                pool.wait_ge(y_stored[s], (TILES + 1 - s) // 2 * 16)
            for b in range(NB):
                s = b % NG
                if b >= NG:
                    pool.wait_ge(out_ready, b - NG + 1)
                for k in range(TOPK):
                    pool.indirect_dma_start(y_in[0:LQ, s, k], None, sorted_y, bass.IndirectOffsetOnAxis(ap=slot_i[0:LQ, k, b:b + 1], axis=0)).then_inc(gathered[s], 16)

        @block.scalar
        def _(act):
            act.wait_ge(tanh_loaded, 16)
            act.activation(tanh_f[:, :], tanh_f[:, :], ACT.Tanh).then_inc(act_done, 1)
            act.wait_ge(ratio_ready, 1)
            act.activation(ratio[0:LQ, 1], ratio[0:LQ, 0], ACT.Exp).then_inc(act_done, 1)

            def body(t):
                if t.has(0):
                    for n in range(2):
                        act.wait_ge(biased, t(2, n + 1))
                        if t.at >= 1:
                            act.wait_ge(ht_done, t(2))
                        act.activation(g_sb[:, n], h_sb[:, n], ACT.Gelu).then_inc(gelu_done, 1)
                    act.wait_ge(ht_done, t(2, 1))
                    if t.at >= 1:
                        act.wait_ge(y_done, t(1))
                    act.activation(ht_sb[:, 0:4], ht_ps[0][:, :].rearrange("p (c t) -> p c t", c=4), ACT.Copy).then_inc(ht_copied[0], 1)

            tiles(act, body)

        @block.vector
        def _(dve):
            n_step = [0]

            def then(instruction):
                n_step[0] += 1
                instruction.then_inc(step, 1)
                dve.wait_ge(step, n_step[0])

            L = slice(0, LQ)
            then(dve.tensor_tensor(ratio[L, 0], top_v[L, :, 1], top_v[L, :, 0], ALU.subtract))
            dve.sem_inc(ratio_ready, 1)
            dve.wait_ge(act_done, 2)
            then(dve.tensor_scalar(ratio[L, 2], ratio[L, 1], 1.0, None, ALU.add))
            then(dve.reciprocal(weight[L, 0], ratio[L, 2]))
            then(dve.tensor_tensor(weight[L, 1], weight[L, 0], ratio[L, 1], ALU.mult))
            then(dve.tensor_scalar(weight[L, :, :], weight[L, :, :], tanh_f[L, :], None, ALU.mult))
            then(dve.tensor_copy(top_f[L, :, :], top_i[L, :, 0:TOPK].rearrange("p b k -> p k b")))
            for e in range(E):
                last = dve.tensor_scalar(onehot[L, e], top_f[L, :, :], float(e), None, ALU.is_equal)
            then(last)
            dve.tensor_tensor(member[L, :, :], onehot[L, :, 0], onehot[L, :, 1], ALU.add).then_inc(counted, 1)
            dve.wait_ge(counted, 2)
            flat = lambda a: a.rearrange("p e b -> p (e b)")
            then(dve.tensor_copy(flat(total[L, :, :]), count_ps[L, E * NB:2 * E * NB]))
            then(dve.tensor_reduce(count_f[L, :], total[L, :, :], AX.X, ALU.add))
            then(dve.tensor_scalar(count_i[L, 0], count_f[L, :], 127.0, None, ALU.add))
            then(dve.tensor_scalar(count_i[L, 1], count_i[L, 0], 7, None, ALU.arith_shift_right))
            then(dve.tensor_copy(tiles_f[L, :], count_i[L, 1]))
            then(dve.tensor_tensor_scan(tile_end[L, :], ones[L, 0:E], tiles_f[L, :], 0.0, ALU.mult, ALU.add))
            then(dve.tensor_tensor(slot_start[L, :], tile_end[L, :], tiles_f[L, :], ALU.subtract))
            then(dve.tensor_scalar(slot_start[L, :], slot_start[L, :], 128.0, None, ALU.mult))
            for e in range(E):
                last = dve.tensor_tensor_scan(slot[L, e], ones[L, 0:NB], total[L, e], slot_start[L, e:e + 1], ALU.mult, ALU.add)
            then(last)
            then(dve.tensor_tensor(slot[L, :, :], slot[L, :, :], total[L, :, :], ALU.subtract))
            then(dve.tensor_tensor(flat(slot[L, :, :]), flat(slot[L, :, :]), count_ps[L, 0:E * NB], ALU.add))
            for k in range(TOPK):
                last = dve.tensor_tensor(picked[L, k], slot[L, :, :], onehot[L, :, k], ALU.mult)
            then(last)
            for k in range(TOPK):
                last = dve.tensor_reduce(slot_f[L, k], picked[L, k].rearrange("p e b -> p b e"), AX.X, ALU.add)
            then(last)
            then(dve.tensor_copy(slot_i[L, :, :], slot_f[L, :, :]))
            dve.sem_inc(slots_ready, 1)
            for e in range(E - 1):
                if e == 0:
                    then(dve.tensor_scalar(tile_acc[:, 0], tile_no[:, :], tile_end[0:1, 0:1], None, ALU.is_ge))
                else:
                    then(dve.scalar_tensor_tensor(out=tile_acc[:, e % 2], in0=tile_no[:, :], scalar=tile_end[0:1, e:e + 1], in1=tile_acc[:, (e - 1) % 2],
                                                  op0=ALU.is_ge, op1=ALU.add))
            then(dve.tensor_copy(tile_expert[:, :], tile_acc[:, (E - 2) % 2]))
            dve.sem_inc(slots_ready, 1)
            dve.wait_ge(weights_loaded, 16 * (2 * E + 2))

            def body(t):
                if t.has(0):
                    ex = dve.value_load(tile_expert[0:1, bass.ds(t(1), 1)] if t.i is not None else tile_expert[0:1, t.at:t.at + 1], min_val=0, max_val=E - 1)
                    bias1 = lambda n: b1_sb[:, bass.ds(ex, 1), n * 512:n * 512 + 512].rearrange("p o f -> p (o f)")
                    for n in range(2):
                        dve.wait_ge(h_done, t(2, n + 1))
                        if t.at >= 1:
                            dve.wait_ge(gelu_done, t(2, n - 1))
                        dve.tensor_tensor(h_sb[:, n], h_ps[n][:, :], bias1(n), ALU.add).then_inc(biased, 1)
                    dve.wait_ge(ht_done, t(2, 2))
                    if t.at >= 1:
                        dve.wait_ge(y_done, t(1))
                    dve.tensor_copy(ht_sb[:, 4:8], ht_ps[1][:, :].rearrange("p (c t) -> p c t", c=4)).then_inc(ht_copied[1], 1)
                if t.has(2):
                    dve.wait_ge(xt_done, t(1, 3))
                    dve.tensor_copy(xt_sb[:, t.at % 2], xt_ps[:, 0:KD * 128].rearrange("p (k t) -> p k t", k=KD)).then_inc(xt_copied, 1)
                if t.has(0):
                    dve.wait_ge(y_done, t(1, 1))
                    if t.at >= 2:
                        dve.wait_ge(y_stored[t.at % 2], t.halves(16, -2))
                    dve.tensor_tensor(y_sb[:, t.at % 2], y_ps[:, 0:D], b2_sb[:, bass.ds(ex, 1), :].rearrange("p o d -> p (o d)"), ALU.add).then_inc(y_ready, 1)

            tiles(dve, body)
            for b in range(NB):
                s = b % NG
                dve.wait_ge(gathered[s], (b // NG + 1) * 32)
                dve.wait_ge(x2_loaded[s], (b // NG + 1) * 16)
                dve.scalar_tensor_tensor(out=part_sb[L, s], in0=y_in[L, s, 0], scalar=weight[L, 0, b:b + 1], in1=x2_sb[L, s], op0=ALU.mult, op1=ALU.add).then_inc(part_done, 1)
                dve.wait_ge(part_done, b + 1)
                if b >= NG:
                    dve.wait_ge(out_stored[s], b // NG * 16)
                dve.scalar_tensor_tensor(out=o_sb[L, s], in0=y_in[L, s, 1], scalar=weight[L, 1, b:b + 1], in1=part_sb[L, s], op0=ALU.mult, op1=ALU.add).then_inc(out_ready, 1)

        @block.tensor
        def _(pe):
            pe.wait_ge(made, 5)
            pe.wait_ge(counted, 1)
            rows = member[0:LQ, :, :].rearrange("p e b -> p (e b)")
            nc.tensor.matmul(count_ps[0:LQ, 0:E * NB], before_me[0:LQ, 0:LQ], rows, start=True, stop=True)
            nc.tensor.matmul(count_ps[0:LQ, E * NB:2 * E * NB], ones[0:LQ, 0:LQ], rows, start=True, stop=True).then_inc(counted, 1)
            pe.wait_ge(slots_ready, 2)
            pe.wait_ge(weights_loaded, 16 * (2 * E + 1))

            def body(t):
                if t.has(1):
                    e1 = pe.value_load(tile_expert[0:1, bass.ds(t(1, 1), 1)] if t.i is not None else tile_expert[0:1, t.at + 1:t.at + 2], min_val=0, max_val=E - 1)
                for n in range(2):
                    if t.has(1):
                        if n == 0:
                            pe.wait_ge(xt_copied, t(1, 2))
                        if t.at >= 0:
                            pe.wait_ge(biased, t(2, n + 1))
                        for k in range(KD):
                            last = nc.tensor.matmul(h_ps[n][:, :], xt_sb[:, (t.at + 1) % 2, k],
                                                    w1_sb[:, k, bass.ds(e1, 1), n * 512:n * 512 + 512].rearrange("p o f -> p (o f)"), start=(k == 0), stop=(k == KD - 1))
                        last.then_inc(h_done, 1)
                    if n == 0 and t.has(0):
                        for m in range(2):
                            pe.wait_ge(gelu_done, t(2, m + 1))
                            if t.at >= 1:
                                pe.wait_ge(ht_copied[m], t(1))
                            for c in range(4):
                                last = nc.tensor.transpose(ht_ps[m][:, c * 128:c * 128 + 128], g_sb[:, m, c * 128:c * 128 + 128], ident2[:, :])
                            last.then_inc(ht_done, 1)
                if t.has(2):
                    pe.wait_ge(x_loaded[t.at % 2], t.halves(16, 2))
                    if t.at >= -1:
                        pe.wait_ge(xt_copied, t(1, 2))
                    for k in range(KD):
                        last = nc.tensor.transpose(xt_ps[:, k * 128:k * 128 + 128], x_sb[:, t.at % 2, k * 128:k * 128 + 128], ident2[:, :])
                    last.then_inc(xt_done, 1)
                if t.has(0):
                    e0 = pe.value_load(tile_expert[0:1, bass.ds(t(1), 1)] if t.i is not None else tile_expert[0:1, t.at:t.at + 1], min_val=0, max_val=E - 1)
                    for m in range(2):
                        pe.wait_ge(ht_copied[m], t(1, 1))
                    if t.at >= 1:
                        pe.wait_ge(y_ready, t(1))
                    for c in range(KF):
                        last = nc.tensor.matmul(y_ps[:, 0:D], ht_sb[:, c], w2_sb[:, c, bass.ds(e0, 1), :].rearrange("p o d -> p (o d)"), start=(c == 0), stop=(c == KF - 1))
                    last.then_inc(y_done, 1)

            tiles(pe, body)


def program(nc, x, ctx, g_x, g_f, ln_m_g, ln_m_b, ln_l_g, ln_l_b, wq, wkv, wout, gate_w, w1, b1, w2, b2, out):
    dram = lambda name, shape: nc.dram_tensor(name, shape, F32).ap()
    x2_dram = dram("x2_dram", [NB, LQ, D])
    xn_dram = dram("xn_dram", [NB, LQ, D])
    sorted_x = dram("sorted_x", [TILES * 128, D])
    sorted_y = dram("sorted_y", [TILES * 128, D])
    with ExitStack() as st:
        top_v = st.enter_context(nc.sbuf_tensor("top_v", [128, NB, TOPK], F32))
        top_i = st.enter_context(nc.sbuf_tensor("top_i", [128, NB, TOPK], U32))
        with ExitStack() as inner:
            ident = inner.enter_context(nc.sbuf_tensor("ident", [128, 128], F32))
            attention(nc, x, ctx, g_x, ln_m_g, ln_m_b, ln_l_g, ln_l_b, wq, wkv, wout, gate_w, x2_dram, xn_dram, top_v, top_i, ident, sorted_x)
        routed_ffn(nc, g_f, w1, b1, w2, b2, x2_dram, xn_dram, out, sorted_x, sorted_y, top_v, top_i)


_INS = ['x', 'ctx_1024', 'g_xattn', 'g_ffn', 'L0_xattn_ln_m_g', 'L0_xattn_ln_m_b', 'L0_xattn_ln_l_g', 'L0_xattn_ln_l_b',
        'L0_xattn_Wq', 'L0_xattn_Wkv', 'L0_xattn_Wout', 'L0_ffn_gate_w', 'L0_ffn_w1', 'L0_ffn_b1', 'L0_ffn_w2', 'L0_ffn_b2']
_OUTS = [((NB, LQ, D), 'float32')]


def kernel(**inputs):
    import numpy as _np
    import concourse.bacc as _bacc
    from concourse import mybir as _mybir
    from concourse.bass_utils import run_bass_kernel_spmd as _run

    nc = _bacc.Bacc("TRN2", target_bir_lowering=False, num_devices=1)
    arrays, args = {}, []
    for name in _INS:
        a = _np.ascontiguousarray(inputs[name])
        arrays[f"in_{name}_dram"] = a
        args.append(nc.dram_tensor(f"in_{name}_dram", a.shape, _mybir.dt.from_np(a.dtype), kind="ExternalInput").ap())
    for i, (shape, dtype) in enumerate(_OUTS):
        dt = _mybir.dt.from_np(_np.dtype(dtype))
        args.append(nc.dram_tensor(f"out_{i}_dram", shape, dt, kind="ExternalOutput").ap())
    program(nc, *args)
    r = _run(nc, [arrays], core_ids=[0])
    got = tuple(r.results[0][f"out_{i}_dram"] for i in range(len(_OUTS)))
    return got[0]
```

```python
import concourse.bass as bass
from concourse import mybir
from contextlib import ExitStack

F32 = mybir.dt.float32
F32R = mybir.dt.float32r
I32 = mybir.dt.int32
U32 = mybir.dt.uint32
ALU = mybir.AluOpType
ACT = mybir.ActivationFunctionType
AX = mybir.AxisListType

NB, LQ, LC, D = 32, 112, 375, 256
H, DH = 16, 64
LK = LC + LQ
LKP = LK + LK % 2
KD = D // 128
CT, CP = 3, LC // 3
NP = H // 2
KT = 4
INNER = H * DH
E, TOPK, F = 8, 2, 1024
EPS = 1e-5
TILES = (NB * LQ * TOPK + E * 127) // 128
UNITS = 20


class Batch:

    def __init__(self, at, i=None, step=0):
        self.at, self.i, self.step = at, i, step

    def __call__(self, per, extra=0):
        fixed = self.at * per + extra
        return fixed if self.i is None else self.i * (self.step * per) + fixed

    def has(self, offset):
        return self.i is not None or 0 <= self.at + offset < NB

    def halves(self, offset, per):
        fixed = per * ((self.at + offset) // 2 + 1)
        return fixed if self.i is None else self.i * (self.step // 2 * per) + fixed

    def parity(self, offset):
        return (self.at + offset) % 2


def batches(engine, body):
    for b in range(-2, 3):
        body(Batch(b))
    with engine.Fori(0, (NB - 6) // 2) as i:
        body(Batch(3, i, 2))
        body(Batch(4, i, 2))
    for b in range(NB - 3, NB + 1):
        body(Batch(b))


def units_of(b):
    if b.i is None and not -2 <= b.at <= NB:
        return []
    found = []
    kq, v = 0, 0
    for j in range(NP):
        if b.has(1):
            found.append(("K", j, b(10, 10 + kq + 1)))
            kq += 1
            found.append(("V", j, b(8, 8 + v + 1)))
            v += 1
        if b.has(2) and j in (4, 6):
            found.append(("T", (j - 4) // 2, b(2, 4 + (j - 4) // 2 + 1)))
        if b.has(1) and j in (5, 7):
            found.append(("Q", (j - 5) // 2, b(10, 10 + kq + 1)))
            kq += 1
    return found


def first_unit(b):
    if b.i is None and b.at == -2:
        return 0
    return b(UNITS, 2 + UNITS)


def before(b):
    return Batch(b.at - 1, b.i, b.step)


def lag_batch(b):
    return b.i is not None or b.at >= 1


def prev_pair(b, j):
    return b.has(0) if j >= 1 else lag_batch(b)


def pv_pair(b, j):
    return b.has(0) if j >= 2 else lag_batch(b)


def o_pair(b, j):
    return b.has(0) if j >= 3 else lag_batch(b)


def unit_number(b, kind, index):
    n = [u[:2] for u in units_of(b)].index((kind, index))
    return first_unit(b) + n + 1, (n + first_unit(Batch(0))) % 2


def attention(nc, x, ctx_in, g_x, ln_m_g, ln_m_b, ln_l_g, ln_l_b, wq, wkv, wout, gate_w, x2_out, xn_out, top_v, top_i, ident, sorted_x):
    with ExitStack() as st:
        sb = lambda name, shape, dt=F32: st.enter_context(nc.sbuf_tensor(name, shape, dt))
        sem = lambda name: st.enter_context(nc.semaphore(name))
        bank = lambda name: st.enter_context(nc.psum_tensor(name, [128, 512], F32))

        wkv_hi = sb("wkv_hi", [128, KD, 2 * INNER], F32R)
        wkv_lo = sb("wkv_lo", [128, KD, 2 * INNER], F32R)
        wq_sb = sb("wq_sb", [128, KD, INNER])
        wout_hi = sb("wout_hi", [128, NP, D], F32R)
        wout_lo = sb("wout_lo", [128, NP, D], F32R)
        gate_sb = sb("gate_sb", [128, KD, E])
        affine = sb("affine", [128, 4, KD])
        tanh_g = sb("tanh_g", [128, 1])
        ctx_sb = sb("ctx_sb", [128, 2, CT, D])
        x_sb = sb("x_sb", [128, 2, D])
        norm_sb = sb("norm_sb", [128, CT + 1, D])
        stats = sb("stats", [128, CT + 1, 6])
        moments = sb("moments", [128, CT + 1, 2])
        rstd = sb("rstd", [128, 4 * (CT + 1)])
        half = sb("half", [128, CT + 1])
        eps = sb("eps", [128, CT + 1])
        kv_f = sb("kv_f", [128, KD, LKP])
        lat_f = sb("lat_f", [128, 2, KD, LQ])
        kv_hi = sb("kv_hi", [128, 2, KD, LKP], F32R)
        kv_lo = sb("kv_lo", [128, 2, KD, LKP], F32R)
        q_hi = sb("q_hi", [128, H, LQ], F32R)
        q_lo = sb("q_lo", [128, H, LQ], F32R)
        k_both = sb("k_both", [128, H, LKP], F32R)
        v_sb = sb("v_sb", [128, 2, KT, INNER])
        p_sb = sb("p_sb", [128, 2, 2, 512])
        pt_sb = sb("pt_sb", [128, 2, 2, KT, LQ])
        neg_max = sb("neg_max", [128, 2, 2])
        row_sum = sb("row_sum", [128, 2, 2])
        inv_sum = sb("inv_sum", [128, 2, 2])
        o_hi = sb("o_hi", [128, 2, NP, LQ], F32R)
        o_lo = sb("o_lo", [128, 2, NP, LQ], F32R)
        res_sb = sb("res_sb", [128, 2, D])
        x2_sb = sb("x2_sb", [128, 2, D])
        xn_sb = sb("xn_sb", [128, 2, D])
        stats2 = sb("stats2", [128, 6])
        moments2 = sb("moments2", [128, 2])
        rstd2 = sb("rstd2", [128, 2])
        xnt_sb = sb("xnt_sb", [128, KD, LQ])
        logits_sb = sb("logits_sb", [128, E])
        max_v = sb("max_v", [128, 8])
        max_i = sb("max_i", [128, 8], U32)
        zero_sb = sb("zero_sb", [128, D])

        scores_ps = [bank("scores_ps0"), bank("scores_ps1")]
        pt_ps = [bank("pt_ps0"), bank("pt_ps1")]
        proj_ps = [bank("proj_ps0"), bank("proj_ps1")]
        pv_ps = bank("pv_ps")
        tail_ps = bank("tail_ps")

        w_loaded = sem("w_loaded"); small_loaded = sem("small_loaded")
        zeroed = sem("zeroed")
        w_hi_done = sem("w_hi_done"); w_ready = sem("w_ready"); set_up = sem("set_up"); tanh_done = sem("tanh_done")
        ctx_loaded = [sem("ctx_loaded0"), sem("ctx_loaded1")]
        res_loaded = [sem("res_loaded0"), sem("res_loaded1")]
        stats_done = sem("stats_done"); moments_done = sem("moments_done"); rstd_done = sem("rstd_done"); pool_step = sem("pool_step")
        norm_done = sem("norm_done")
        proj_done = sem("proj_done"); kq_hi = sem("kq_hi"); q_copied = sem("q_copied"); kq_lo = sem("kq_lo"); v_copied = sem("v_copied")
        kv_affine = sem("kv_affine"); kvhi_done = sem("kvhi_done"); kvlo_done = sem("kvlo_done")
        scores_done = sem("scores_done"); max_done = sem("max_done"); exp_done = sem("exp_done"); inv_done = sem("inv_done"); p_ready = sem("p_ready")
        pt_done = sem("pt_done"); pt_copied = [sem("pt_copied_act"), sem("pt_copied_dve")]
        pv_done = sem("pv_done"); o_high = sem("o_high"); o_copied = sem("o_copied")
        out_done = sem("out_done"); x2_done = sem("x2_done"); stats2_done = sem("stats2_done"); rstd2_done = sem("rstd2_done")
        xn_done = sem("xn_done"); xnt_done = sem("xnt_done"); xnt_copied = sem("xnt_copied"); logits_done = sem("logits_done")
        logits_copied = sem("logits_copied"); top_done = sem("top_done"); stored = [sem("stored0"), sem("stored1")]

        block = st.enter_context(nc.Block())

        v_flat = v_sb[:, :, :, :].rearrange("p a b c -> p (a b c)")
        stage = v_flat[:, 0:KD * 2 * INNER].rearrange("p (k n) -> p k n", k=KD)
        stage_out = v_flat[:, KD * 2 * INNER:KD * 2 * INNER + NP * D].rearrange("p (j n) -> p j n", j=NP)

        @block.sync
        def _(sp):
            sp.dma_start(stage, wkv.rearrange("(k p) n -> p k n", p=128)).then_inc(w_loaded, 16)
            for n, a in enumerate((ln_m_g, ln_m_b, ln_l_g, ln_l_b)):
                sp.dma_start(affine[:, n, :], a.rearrange("(k p) -> p k", p=128), allow_slow_non_contiguous=True).then_inc(small_loaded, 16)
            sp.dma_start(tanh_g[:, :], g_x.partition_broadcast(128)).then_inc(small_loaded, 16)
            sp.dma_start(gate_sb[:, :, :], gate_w.rearrange("(k p) e -> p k e", p=128)).then_inc(small_loaded, 16)

            def load(b, off):
                s = b.parity(off)
                c = b(1, off)
                cx = ctx_in[c] if isinstance(c, int) else ctx_in[bass.ds(c, 1)].rearrange("o n d -> (o n) d")
                xx = x[c] if isinstance(c, int) else x[bass.ds(c, 1)].rearrange("o n d -> (o n) d")
                sp.dma_start(ctx_sb[0:CP, s], cx.rearrange("(t p) d -> p t d", p=CP)).then_inc(ctx_loaded[s], 16)
                sp.dma_start(x_sb[0:LQ, s], xx).then_inc(ctx_loaded[s], 16)

            load(Batch(0), 0)
            load(Batch(0), 1)
            sp.dma_start(wq_sb[:, :, :], wq.rearrange("(k p) n -> p k n", p=128)).then_inc(small_loaded, 16)
            sp.dma_start(stage_out, wout.rearrange("(j p) n -> p j n", p=128)).then_inc(small_loaded, 16)

            sp.wait_ge(set_up, 1)
            slots = sorted_x.rearrange("(t p) d -> p t d", p=128)
            for t in range(0, TILES, 9):
                sp.dma_start(slots[:, t:t + 9], zero_sb[:, None, :].broadcast_to((128, 9, D))).then_inc(zeroed, 16)

            def body(b):
                if b.has(3) and not (b.i is None and b.at < -1):
                    sp.wait_ge(norm_done, b(1, 2))
                    load(b, 3)
                if b.has(0):
                    s = b.parity(0)
                    if b.at >= 2:
                        sp.wait_ge(x2_done, b(1, -1))
                    c = b(1)
                    xx = x[c] if isinstance(c, int) else x[bass.ds(c, 1)].rearrange("o n d -> (o n) d")
                    sp.dma_start(res_sb[0:LQ, s], xx).then_inc(res_loaded[s], 16)
                if b.has(-1) and not (b.i is None and b.at < 1):
                    s = b.parity(-1)
                    c = b(1, -1)
                    o1, o2 = (t[c] if isinstance(c, int) else t[bass.ds(c, 1)].rearrange("o n d -> (o n) d") for t in (x2_out, xn_out))
                    sp.wait_ge(x2_done, b(1))
                    sp.dma_start(o1, x2_sb[0:LQ, s]).then_inc(stored[s], 16)
                    sp.wait_ge(xn_done, b(1))
                    sp.dma_start(o2, xn_sb[0:LQ, s]).then_inc(stored[s], 16)

            batches(sp, body)
            for s in stored:
                sp.wait_ge(s, NB // 2 * 32)
            sp.wait_ge(zeroed, 16 * (TILES // 9))

        @block.gpsimd
        def _(pool):
            pool.memset(ident[:, :], 0.0).then_inc(pool_step, 1)
            pool.memset(half[:, :], -0.5).then_inc(pool_step, 1)
            pool.wait_ge(pool_step, 2)
            pool.affine_select(out=ident[:, :], in_=ident[:, :], compare_op=ALU.not_equal, fill=1.0, base=0,
                               pattern=[[-1, 128]], channel_multiplier=1).then_inc(pool_step, 1)
            pool.memset(kv_f[:, :, LK:LKP], 0.0).then_inc(pool_step, 1)
            for s in range(2):
                for h in range(2):
                    pool.memset(p_sb[0:LQ, s, h, LK:512], 0.0).then_inc(pool_step, 1)
            pool.memset(moments[:, :, :], 1.0).then_inc(pool_step, 1)
            pool.memset(zero_sb[:, :], 0.0).then_inc(pool_step, 1)
            pool.memset(eps[:, :], EPS).then_inc(pool_step, 1)
            pool.wait_ge(pool_step, 11)
            pool.sem_inc(set_up, 1)

            N = CT + 1
            r = lambda a, k=None: rstd[0:CP, a * N:(a + 1) * N] if k is None else rstd[0:LQ, a * N + CT:a * N + CT + 1]
            COUNT = 8

            def normalise(b, op, done):
                s = b.parity(2)
                rows_c = ctx_sb[0:CP, s] if op == ALU.subtract else norm_sb[0:CP, 0:CT]
                rows_l = x_sb[0:LQ, s] if op == ALU.subtract else norm_sb[0:LQ, CT]
                if op == ALU.subtract:
                    col_c, col_l = moments[0:CP, 0:CT, 0:1], moments[0:LQ, CT, 0:1]
                else:
                    col_c, col_l = rstd[0:CP, CT + 1:2 * CT + 1][:, :, None], rstd[0:LQ, 2 * CT + 1:2 * CT + 2]
                pool.tensor_tensor(norm_sb[0:CP, 0:CT], rows_c, col_c.broadcast_to((CP, CT, D)), op)
                pool.tensor_tensor(norm_sb[0:LQ, CT], rows_l, col_l.broadcast_to((LQ, D)), op).then_inc(done, 1)

            def body(b):
                step = lambda n: b(COUNT, 2 * COUNT + 11 + n)
                s = b.parity(2)
                for j in range(NP):
                    if b.has(0):
                        for h in range(2):
                            pool.wait_ge(inv_done, b(H, 2 * j + h + 1))
                            p = p_sb[0:LQ, j % 2, h, 0:LK]
                            pool.tensor_tensor(p, p, inv_sum[0:LQ, j % 2, h:h + 1].broadcast_to((LQ, LK)), ALU.mult).then_inc(p_ready, 1)
                    if b.has(2) and j == 1:
                        pool.wait_ge(moments_done, b(1, 3))
                        pool.tensor_tensor(r(0), moments[0:CP, :, 1], eps[0:CP, :], ALU.add).then_inc(pool_step, 1)
                        pool.wait_ge(pool_step, step(1))
                        pool.tensor_tensor(r(1), r(0), half[0:CP, :], ALU.pow).then_inc(pool_step, 1)
                        pool.wait_ge(pool_step, step(2))
                        pool.tensor_tensor(r(2, 1), r(1, 1), r(1, 1), ALU.mult).then_inc(pool_step, 1)
                        pool.wait_ge(pool_step, step(3))
                        pool.tensor_tensor(r(3, 1), r(2, 1), moments[0:LQ, CT:CT + 1, 1], ALU.mult).then_inc(pool_step, 1)
                        pool.wait_ge(pool_step, step(4))
                        pool.tensor_tensor(r(2, 1), r(3, 1), eps[0:LQ, 0:1], ALU.add).then_inc(pool_step, 1)
                        pool.wait_ge(pool_step, step(5))
                        pool.tensor_tensor(r(3, 1), r(2, 1), half[0:LQ, 0:1], ALU.pow).then_inc(pool_step, 1)
                        pool.wait_ge(pool_step, step(6))
                        pool.tensor_tensor(r(1, 1), r(1, 1), r(3, 1), ALU.mult).then_inc(pool_step, 1)
                    if b.has(2) and j == 2:
                        pool.wait_ge(pool_step, step(7))
                        if b.i is not None or b.at > -2:
                            pool.wait_ge(kv_affine, b(2, 4))
                        normalise(b, ALU.subtract, pool_step)
                    if b.has(2) and j == 3:
                        pool.wait_ge(pool_step, step(8))
                        normalise(b, ALU.mult, norm_done)
                    if lag_batch(b) and j == 3:
                        pool.wait_ge(stats2_done, b(2))
                        pool.tensor_tensor(rstd2[0:LQ, 0:1], moments2[0:LQ, 1:2], eps[0:LQ, 0:1], ALU.add).then_inc(rstd2_done, 1)
                        pool.wait_ge(rstd2_done, b(2, -1))
                        pool.tensor_tensor(rstd2[0:LQ, 1:2], rstd2[0:LQ, 0:1], half[0:LQ, 0:1], ALU.pow).then_inc(rstd2_done, 1)
                    if b.has(2) and j in (5, 7):
                        k = (j - 5) // 2
                        pool.wait_ge(kvhi_done, b(2, 4 + k + 1))
                        pool.tensor_tensor(kv_lo[:, s, k], kv_f[:, k], kv_hi[:, s, k].bitcast(F32), ALU.subtract).then_inc(kvlo_done, 1)

            batches(pool, body)

        @block.scalar
        def _(act):
            act.wait_ge(small_loaded, 16 * 8)
            act.activation(tanh_g[:, :], tanh_g[:, :], ACT.Tanh).then_inc(tanh_done, 1)

            def q_high(b, j):
                done, k = unit_number(b, "Q", j)
                act.wait_ge(proj_done, done)
                for r in range(2):
                    last = act.activation(q_hi[0:64, 8 * j + r:8 * j + 8:2], proj_ps[k][64 * r:64 * r + 64, 0:4 * LQ].rearrange("p (m q) -> p m q", m=4),
                                          ACT.Copy, scale=float(DH) ** -0.5)
                last.then_inc(kq_hi, 1)

            def q_again(tensor, j):
                act.activation(tensor[64:128, 8 * j:8 * j + 8], tensor[0:64, 8 * j:8 * j + 8].bitcast(F32), ACT.Copy).then_inc(q_copied, 1)

            def body(b):
                for j in range(NP):
                    if o_pair(b, j):
                        act.wait_ge(pv_done, b(NP, j - 2))
                        act.activation(o_hi[:, b.parity(0 if j >= 3 else -1), (j - 3) % NP], pv_ps[:, 0:LQ], ACT.Copy).then_inc(o_high, 1)
                    if b.has(0) and j == 0:
                        q_high(before(b), 1)
                    if b.has(1) and j == 6:
                        q_high(b, 0)
                    if lag_batch(b) and j == 6:
                        act.wait_ge(xnt_done, b(1))
                        act.activation(xnt_sb[:, :, :], tail_ps[:, 0:KD * LQ].rearrange("p (k q) -> p k q", k=KD), ACT.Copy).then_inc(xnt_copied, 1)
                    if b.has(0):
                        for h in range(2):
                            act.wait_ge(max_done, b(H, 2 * j + h + 1))
                            act.activation(p_sb[0:LQ, j % 2, h, 0:LK], scores_ps[h][0:LQ, 0:LK], ACT.Exp,
                                           bias=neg_max[0:LQ, j % 2, h:h + 1], accum_out=row_sum[0:LQ, j % 2, h:h + 1]).then_inc(exp_done, 1)
                    if b.has(1):
                        done, k = unit_number(b, "K", j)
                        act.wait_ge(proj_done, done)
                        for r in range(2):
                            last = act.activation(k_both[0:64, 2 * j + r], proj_ps[k][64 * r:64 * r + 64, 0:LKP], ACT.Copy)
                        last.then_inc(kq_hi, 1)
                    if prev_pair(b, j):
                        act.wait_ge(pt_done, b(H, 2 * j - 1))
                        act.activation(pt_sb[:, (j - 1) % 2, 0], pt_ps[0][:, 0:KT * LQ].rearrange("p (t q) -> p t q", t=KT), ACT.Copy).then_inc(pt_copied[0], 1)
                    if b.has(2) and j in (5, 7):
                        k = (j - 5) // 2
                        act.wait_ge(kv_affine, b(2, 4 + k + 1))
                        act.activation(kv_hi[:, b.parity(2), k], kv_f[:, k], ACT.Copy).then_inc(kvhi_done, 1)
                    if b.has(1):
                        done, k = unit_number(b, "V", j)
                        act.wait_ge(proj_done, done)
                        t, half_ = j % KT, j // KT
                        rows = 128 if t < KT - 1 else LKP - 128 * (KT - 1)
                        if b.i is None and b.at == -1 and j == 0:
                            act.wait_ge(w_ready, 2)
                        act.activation(v_sb[0:rows, b.parity(1), t, half_ * 512:half_ * 512 + 512], proj_ps[k][0:rows, :], ACT.Copy).then_inc(v_copied, 1)
                    if b.has(1) and j == 6:
                        act.wait_ge(kq_hi, b(10, 10 + 7))
                        q_again(q_hi, 0)
                    if b.has(1) and j == 7:
                        act.wait_ge(kq_lo, b(10, 10 + 7))
                        q_again(q_lo, 0)
                    if b.has(0) and j == 0:
                        act.wait_ge(kq_hi, b(10, 10))
                        q_again(q_hi, 1)
                    if b.has(0) and j == 1:
                        act.wait_ge(kq_lo, b(10, 10))
                        q_again(q_lo, 1)

            batches(act, body)

        @block.vector
        def _(dve):
            dve.wait_ge(w_loaded, 16)
            for k in range(KD):
                dve.tensor_copy(wkv_hi[:, k], stage[:, k]).then_inc(w_hi_done, 1)
            for k in range(KD):
                dve.wait_ge(w_hi_done, k + 1)
                dve.tensor_tensor(wkv_lo[:, k], stage[:, k], wkv_hi[:, k].bitcast(F32), ALU.subtract).then_inc(w_hi_done, 1)
            dve.wait_ge(small_loaded, 16 * 8)
            dve.tensor_copy(wout_hi[:, :, :], stage_out).then_inc(w_hi_done, 1)
            dve.wait_ge(w_hi_done, 5)
            dve.tensor_tensor(wout_lo[:, :, :], stage_out, wout_hi[:, :, :].bitcast(F32), ALU.subtract).then_inc(w_hi_done, 1)
            dve.wait_ge(w_hi_done, 6)
            for s in range(2):
                dve.memset(v_sb[96:128, s, KT - 1], 0.0).then_inc(w_ready, 1)
            dve.wait_ge(set_up, 1)
            dve.wait_ge(small_loaded, 16 * 8)
            dve.wait_ge(tanh_done, 1)

            def q_low(b, j):
                dve.wait_ge(kq_hi, b(10, 10 + (7 if j == 0 else 10)))
                k = unit_number(b, "Q", j)[1]
                for r in range(2):
                    last = dve.scalar_tensor_tensor(out=q_lo[0:64, 8 * j + r:8 * j + 8:2], in0=proj_ps[k][64 * r:64 * r + 64, 0:4 * LQ].rearrange("p (m q) -> p m q", m=4),
                                                    scalar=float(DH) ** -0.5, in1=q_hi[0:64, 8 * j + r:8 * j + 8:2].bitcast(F32), op0=ALU.mult, op1=ALU.subtract)
                last.then_inc(kq_lo, 1)

            def body(b):
                s = b.parity(2)
                sl = b.parity(-1)
                for j in range(NP):
                    if lag_batch(b) and j == 3:
                        dve.wait_ge(out_done, b(1))
                        dve.wait_ge(res_loaded[sl], b.halves(-1, 16))
                        if b.i is not None or b.at >= 3:
                            dve.wait_ge(stored[sl], b.halves(-3, 32))
                        dve.scalar_tensor_tensor(out=x2_sb[0:LQ, sl], in0=tail_ps[0:LQ, 0:D], scalar=tanh_g[0:LQ, 0:1], in1=res_sb[0:LQ, sl],
                                                 op0=ALU.mult, op1=ALU.add).then_inc(x2_done, 1)
                        dve.wait_ge(x2_done, b(1))
                        dve.bn_stats(stats2[0:LQ, :], x2_sb[0:LQ, sl]).then_inc(stats2_done, 1)
                    if lag_batch(b) and j == 7:
                        dve.wait_ge(logits_done, b(1))
                        dve.tensor_copy(logits_sb[0:LQ, :], tail_ps[0:LQ, 256:256 + E]).then_inc(logits_copied, 1)
                    if b.has(2) and j == 1:
                        dve.wait_ge(stats_done, b(CT + 1, 3 * (CT + 1)))
                    if lag_batch(b) and j == 3:
                        dve.wait_ge(stats2_done, b(2, -1))
                    if lag_batch(b) and j == 7:
                        dve.wait_ge(logits_copied, b(1))
                    if b.has(0):
                        for h in range(2):
                            dve.wait_ge(scores_done, b(H, 2 * j + h + 1))
                            dve.tensor_reduce(neg_max[0:LQ, j % 2, h:h + 1], scores_ps[h][0:LQ, 0:LK], AX.X, ALU.max, negate=True).then_inc(max_done, 1)
                    if b.has(2) and j == 1:
                        for t in range(CT + 1):
                            n = CP if t < CT else LQ
                            last = dve.bn_aggr(moments[0:n, t], stats[0:n, t])
                        last.then_inc(moments_done, 1)
                    if lag_batch(b) and j == 3:
                        dve.bn_aggr(moments2[0:LQ, :], stats2[0:LQ, :]).then_inc(stats2_done, 1)
                    if lag_batch(b) and j == 7:
                        dve.max(max_v[0:LQ, :], logits_sb[0:LQ, :]).then_inc(top_done, 1)
                    if o_pair(b, j):
                        dve.wait_ge(o_high, b(NP, j - 2))
                        dve.tensor_tensor(o_lo[:, b.parity(0 if j >= 3 else -1), (j - 3) % NP], pv_ps[:, 0:LQ],
                                          o_hi[:, b.parity(0 if j >= 3 else -1), (j - 3) % NP].bitcast(F32), ALU.subtract).then_inc(o_copied, 1)
                    if b.has(0) and j == 0:
                        q_low(before(b), 1)
                    if b.has(1) and j == 6:
                        q_low(b, 0)
                    if b.has(2) and j in (5, 7):
                        k = (j - 5) // 2
                        done, n = unit_number(b, "T", k)
                        dve.wait_ge(proj_done, done)
                        if b.i is not None or b.at > -2:
                            dve.wait_ge(kvlo_done, b(2, 2 + k + 1))
                        dve.tensor_scalar(kv_f[:, k, 0:LC], proj_ps[n][:, 0:LC], affine[:, 0, k:k + 1], affine[:, 1, k:k + 1], ALU.mult, ALU.add)
                        dve.tensor_scalar(kv_f[:, k, LC:LK], proj_ps[n][:, LC:LK], affine[:, 2, k:k + 1], affine[:, 3, k:k + 1], ALU.mult, ALU.add)
                        dve.tensor_scalar(lat_f[:, s, k], proj_ps[n][:, LC:LK], affine[:, 2, k:k + 1], affine[:, 3, k:k + 1], ALU.mult, ALU.add).then_inc(kv_affine, 1)
                    if lag_batch(b) and j == 7:
                        dve.wait_ge(top_done, b(2, -1))
                    if b.has(0):
                        for h in range(2):
                            dve.wait_ge(exp_done, b(H, 2 * j + h + 1))
                            dve.reciprocal(inv_sum[0:LQ, j % 2, h:h + 1], row_sum[0:LQ, j % 2, h:h + 1]).then_inc(inv_done, 1)
                    if lag_batch(b) and j == 7:
                        dve.max_index(max_i[0:LQ, :], max_v[0:LQ, :], logits_sb[0:LQ, :]).then_inc(top_done, 1)
                        dve.wait_ge(top_done, b(2))
                    if prev_pair(b, j):
                        dve.wait_ge(pt_done, b(H, 2 * j))
                        dve.tensor_copy(pt_sb[:, (j - 1) % 2, 1], pt_ps[1][:, 0:KT * LQ].rearrange("p (t q) -> p t q", t=KT)).then_inc(pt_copied[1], 1)
                    if b.has(1):
                        idx = 10 + (j + 1 if j < 6 else j + 2)
                        dve.wait_ge(kq_hi, b(10, idx))
                        k = unit_number(b, "K", j)[1]
                        for r in range(2):
                            last = dve.tensor_tensor(k_both[64:128, 2 * j + r], proj_ps[k][64 * r:64 * r + 64, 0:LKP], k_both[0:64, 2 * j + r].bitcast(F32), ALU.subtract)
                        last.then_inc(kq_lo, 1)
                    if b.has(2) and j == 0:
                        dve.wait_ge(ctx_loaded[s], b.halves(2, 32))
                        if b.i is not None or b.at > -2:
                            dve.wait_ge(norm_done, b(1, 2))
                        for t in range(CT + 1):
                            rows = ctx_sb[0:CP, s, t] if t < CT else x_sb[0:LQ, s]
                            dve.bn_stats(stats[0:rows.shape[0], t], rows).then_inc(stats_done, 1)
                    if lag_batch(b) and j == 4:
                        dve.wait_ge(rstd2_done, b(2))
                        dve.tensor_scalar(xn_sb[0:LQ, sl], x2_sb[0:LQ, sl], moments2[0:LQ, 0:1], rstd2[0:LQ, 1:2], ALU.subtract, ALU.mult).then_inc(xn_done, 1)
                    if lag_batch(b) and j == 7:
                        c = b(1, -1)
                        to = lambda t: t[0:LQ, c] if isinstance(c, int) else t[0:LQ, bass.ds(c, 1)].rearrange("p o k -> p (o k)")
                        dve.tensor_copy(to(top_v), max_v[0:LQ, 0:TOPK])
                        dve.tensor_copy(to(top_i), max_i[0:LQ, 0:TOPK])

            batches(dve, body)

        @block.tensor
        def _(pe):
            pe.wait_ge(set_up, 1)

            def free(kind, idx):
                sem_ = {"K": kq_lo, "Q": kq_lo, "V": v_copied, "T": kv_affine}[kind]
                pe.wait_ge(sem_, idx)

            def body(b):
                units = units_of(b)
                earlier = units_of(before(b))[-2:]
                seq = earlier + units
                pos = [0]

                def take():
                    i = pos[0]
                    pos[0] += 1
                    back = i + len(earlier) - 2
                    if back >= 0:
                        free(seq[back][0], seq[back][2])
                    return proj_ps[i % 2]

                def three(out, lhs, rhs):
                    n = 0
                    for k in range(KD):
                        for a, c in ((0, 0), (0, 1), (1, 0)):
                            last = nc.tensor.matmul(out, lhs(a, k), rhs(c, k), start=(n == 0), stop=(n == 3 * KD - 1))
                            n += 1
                    return last

                for j in range(NP):
                    if b.has(0):
                        s = b.parity(0)
                        if j == 0:
                            pe.wait_ge(kq_lo, b(10, 9))
                        if j in (0, 4):
                            pe.wait_ge(q_copied, b(4, 2 if j == 0 else 4))
                        for h in range(2):
                            if j or lag_batch(b):
                                pe.wait_ge(exp_done, b(H, 2 * j + h - 1))
                            for n, part in enumerate((q_hi, q_lo)):
                                last = nc.tensor.matmul(scores_ps[h][0:LQ, 0:LKP], part[:, 2 * j + h], k_both[:, 2 * j + h], start=(n == 0), stop=(n == 1))
                            last.then_inc(scores_done, 1)
                    if b.has(1):
                        s1 = b.parity(1)
                        if j == 0:
                            pe.wait_ge(kvlo_done, b(2, 4))
                            if b.i is None and b.at == -1:
                                pe.wait_ge(w_ready, 2)
                        ps = take()
                        three(ps[:, 0:LKP], lambda a, k: (wkv_hi, wkv_lo)[a][:, k, j * 128:j * 128 + 128],
                              lambda c, k: (kv_hi, kv_lo)[c][:, s1, k]).then_inc(proj_done, 1)
                    if prev_pair(b, j):
                        for h in range(2):
                            pe.wait_ge(p_ready, b(H, 2 * j - 1 + h))
                            if j >= 2 or lag_batch(b):
                                pe.wait_ge(pt_copied[h], b(NP, j - 1))
                            for t in range(KT):
                                last = nc.tensor.transpose(pt_ps[h][:, t * LQ:(t + 1) * LQ], p_sb[0:LQ, (j - 1) % 2, h, t * 128:(t + 1) * 128], ident[0:LQ, 0:LQ])
                            last.then_inc(pt_done, 1)
                    if b.has(1):
                        t, half_ = j % KT, j // KT
                        rows = 128 if t < KT - 1 else LKP - 128 * (KT - 1)
                        ps = take()
                        three(ps[0:rows, :], lambda a, k: (kv_hi, kv_lo)[a][:, s1, k, t * 128:t * 128 + rows],
                              lambda c, k: (wkv_hi, wkv_lo)[c][:, k, INNER + half_ * 512:INNER + half_ * 512 + 512]).then_inc(proj_done, 1)
                    if pv_pair(b, j):
                        p = (j - 2) % NP
                        sv = b.parity(0 if j >= 2 else -1)
                        for h in range(2):
                            pe.wait_ge(pt_copied[h], b(NP, j - 1))
                        if j == 2:
                            pe.wait_ge(v_copied, b(8, 8))
                        if j >= 3 or lag_batch(b):
                            pe.wait_ge(o_copied, b(NP, j - 2))
                        for t in range(KT):
                            for h in range(2):
                                n = 2 * p + h
                                last = nc.tensor.matmul(pv_ps[64 * h:64 * h + 64, 0:LQ], v_sb[:, sv, t, n * DH:(n + 1) * DH], pt_sb[:, (j - 2) % 2, h, t],
                                                        start=(t == 0), stop=(t == KT - 1))
                        last.then_inc(pv_done, 1)
                    if lag_batch(b):
                        sl = b.parity(-1)
                        if j == 2:
                            pe.wait_ge(o_copied, b(NP))
                            if b.i is not None or b.at >= 2:
                                pe.wait_ge(logits_copied, b(1, -1))
                            for p in range(NP):
                                for n, (oo, ww) in enumerate(((o_hi, wout_hi), (o_hi, wout_lo), (o_lo, wout_hi))):
                                    last = nc.tensor.matmul(tail_ps[0:LQ, 0:D], oo[:, sl, p], ww[:, p], start=(p == n == 0), stop=(p == NP - 1 and n == 2))
                            last.then_inc(out_done, 1)
                        if j == 5:
                            pe.wait_ge(xn_done, b(1))
                            for k in range(KD):
                                last = nc.tensor.transpose(tail_ps[:, k * LQ:(k + 1) * LQ], xn_sb[0:LQ, sl, k * 128:(k + 1) * 128], ident[0:LQ, 0:LQ])
                            last.then_inc(xnt_done, 1)
                        if j == 6:
                            pe.wait_ge(xnt_copied, b(1))
                            for k in range(KD):
                                last = nc.tensor.matmul(tail_ps[0:LQ, 256:256 + E], xnt_sb[:, k], gate_sb[:, k], start=(k == 0), stop=(k == KD - 1))
                            last.then_inc(logits_done, 1)
                    if b.has(2) and j in (4, 6):
                        k = (j - 4) // 2
                        if k == 0:
                            pe.wait_ge(norm_done, b(1, 3))
                        ps = take()
                        for t in range(CT):
                            nc.tensor.transpose(ps[:, t * CP:(t + 1) * CP], norm_sb[0:CP, t, k * 128:(k + 1) * 128], ident[0:CP, 0:CP])
                        nc.tensor.transpose(ps[:, LC:LK], norm_sb[0:LQ, CT, k * 128:(k + 1) * 128], ident[0:LQ, 0:LQ]).then_inc(proj_done, 1)
                    if b.has(1) and j in (5, 7):
                        ps = take()
                        for m in range(4):
                            jj = (j - 5) // 2 * 4 + m
                            for k in range(KD):
                                last = nc.tensor.matmul(ps[:, m * LQ:(m + 1) * LQ], wq_sb[:, k, jj * 128:jj * 128 + 128], lat_f[:, s1, k], start=(k == 0), stop=(k == KD - 1))
                        last.then_inc(proj_done, 1)

            batches(pe, body)

def routed_ffn(nc, g_x, w1, b1, w2, b2, x2_in, xn_in, out, sorted_x, sorted_y, top_v, top_i):
    NTOK = NB * TOPK
    with ExitStack() as st:
        sb = lambda name, shape, dt=F32: st.enter_context(nc.sbuf_tensor(name, shape, dt))
        sem = lambda name: st.enter_context(nc.semaphore(name))
        bank = lambda name: st.enter_context(nc.psum_tensor(name, [128, 512], F32))
        KF = F // 128

        w1_sb = sb("w1_sb", [128, KD, E, F])
        w2_sb = sb("w2_sb", [128, KF, E, D])
        b1_sb = sb("b1_sb", [128, E, F])
        xn_all = b1_sb[:, :, :].rearrange("p e f -> p (e f)").rearrange("p (b d) -> p b d", b=NB)
        b2_sb = sb("b2_sb", [128, E, D])
        x_sb = sb("xs_sb", [128, 2, D])
        xt_sb = sb("xt_sb", [128, 2, KD, 128])
        h_sb = sb("h_sb", [128, 2, 512])
        g_sb = sb("g_sb", [128, 2, 512])
        ht_sb = sb("ht_sb", [128, KF, 128])
        y_sb = sb("y_sb", [128, 2, D])
        ident2 = sb("ident2", [128, 128])

        onehot = sb("onehot", [128, E, TOPK, NB])
        member = sb("member", [128, E, NB])
        total = sb("total", [128, E, NB])
        slot = sb("slot", [128, E, NB])
        picked = sb("picked", [128, TOPK, E, NB])
        slot_f = sb("slot_f", [128, TOPK, NB])
        slot_i = sb("slot_i", [128, TOPK, NB], I32)
        top_f = sb("top_f", [128, TOPK, NB])
        count_f = sb("count_f", [128, E])
        count_i = sb("count_i", [128, 2, E], I32)
        tiles_f = sb("tiles_f", [128, E])
        tile_end = sb("tile_end", [128, E])
        slot_start = sb("slot_start", [128, E])
        ones = sb("ones", [128, 128])
        before_me = sb("before_me", [128, 128])
        tile_no = sb("tile_no", [1, TILES])
        tile_acc = sb("tile_acc", [1, 2, TILES])
        tile_expert = sb("tile_expert", [1, TILES], I32)
        weight = sb("weight", [128, TOPK, NB])
        ratio = sb("ratio", [128, 3, NB])
        tanh_f = sb("tanh_f", [128, 1])
        NG = E
        y_in = w1_sb[:, 0, :, 0:TOPK * D].rearrange("p s (k d) -> p s k d", k=TOPK)
        x2_sb, part_sb, o_sb = (w1_sb[:, 1, :, n * D:n * D + D] for n in range(3))

        h_ps = [bank("h_ps0"), bank("h_ps1")]
        ht_ps = [bank("ht_ps0"), bank("ht_ps1")]
        xt_ps = bank("xt_ps")
        y_ps = bank("y_ps")
        count_ps = bank("count_ps")

        made = sem("made"); xn_loaded = sem("xn_loaded"); weights_loaded = sem("weights_loaded"); tanh_loaded = sem("tanh_loaded")
        step = sem("step"); counted = sem("counted"); ratio_ready = sem("ratio_ready"); act_done = sem("act_done")
        slots_ready = sem("slots_ready"); scattered = sem("scattered"); scattered1 = sem("scattered1")
        x_loaded = [sem("xs_loaded0"), sem("xs_loaded1")]
        xt_done = sem("xt_done"); xt_copied = sem("xt_copied"); h_done = sem("h_done"); biased = sem("biased"); gelu_done = sem("gelu_done")
        ht_done = sem("ht_done"); ht_copied = [sem("ht_copied_act"), sem("ht_copied_dve")]
        y_done = sem("y_done"); y_ready = sem("y_ready"); y_stored = [sem("y_stored0"), sem("y_stored1")]
        gathered = [sem(f"gathered{i}") for i in range(NG)]
        x2_loaded = [sem(f"x2_loaded{i}") for i in range(NG)]
        part_done = sem("part_done"); out_ready = sem("out_ready"); out_stored = [sem(f"out_stored{i}") for i in range(NG)]

        block = st.enter_context(nc.Block())
        xs = sorted_x.rearrange("(t p) d -> t p d", p=128)
        ys = sorted_y.rearrange("(t p) d -> t p d", p=128)

        class Tile:
            def __init__(self, at, i=None):
                self.at, self.i = at, i

            def __call__(self, per, extra=0):
                fixed = self.at * per + extra
                return fixed if self.i is None else self.i * (2 * per) + fixed

            def halves(self, per, offset=0):
                fixed = per * ((self.at + offset) // 2 + 1)
                return fixed if self.i is None else self.i * per + fixed

            def has(self, offset):
                return self.i is not None or 0 <= self.at + offset < TILES

        def tiles(engine, body):
            for t in range(-2, 2):
                body(Tile(t))
            n = (TILES - 4) // 2
            with engine.Fori(0, n) as i:
                body(Tile(2, i))
                body(Tile(3, i))
            for t in range(2 + 2 * n, TILES):
                body(Tile(t))

        def row(tensor, c):
            return tensor[c] if isinstance(c, int) else tensor[bass.ds(c, 1)].rearrange("o p d -> (o p) d")

        @block.sync
        def _(sp):
            for n in range(4):
                sp.dma_start(xn_all[0:LQ, n * 8:n * 8 + 8], xn_in[n * 8:n * 8 + 8].rearrange("b p d -> p b d")).then_inc(xn_loaded, 16)
            sp.dma_start(tanh_f[:, :], g_x.partition_broadcast(128)).then_inc(tanh_loaded, 16)
            for e in range(E):
                sp.dma_start(w1_sb[:, :, e], w1[e].rearrange("(k p) f -> p k f", p=128)).then_inc(weights_loaded, 16)
                sp.dma_start(w2_sb[:, :, e], w2[e].rearrange("(k p) d -> p k d", p=128)).then_inc(weights_loaded, 16)
            sp.dma_start(b2_sb[:, :, :], b2.partition_broadcast(128)).then_inc(weights_loaded, 16)
            sp.wait_ge(scattered, 16 * NTOK)
            sp.dma_start(b1_sb[:, :, :], b1.partition_broadcast(128)).then_inc(weights_loaded, 16)

            def body(t):
                if t.has(2):
                    if t.at >= 0:
                        sp.wait_ge(xt_done, t(1, 1))
                    sp.dma_start(x_sb[:, t.at % 2], row(xs, t(1, 2))).then_inc(x_loaded[t.at % 2], 16)
                if t.has(0):
                    sp.wait_ge(y_ready, t(1, 1))
                    sp.dma_start(row(ys, t(1)), y_sb[:, t.at % 2]).then_inc(y_stored[t.at % 2], 16)

            tiles(sp, body)

            def store(b):
                sp.wait_ge(out_ready, b + 1)
                sp.dma_start(out[b], o_sb[0:LQ, b % NG]).then_inc(out_stored[b % NG], 16)

            sp.wait_ge(h_done, 2 * TILES)
            for b in range(NB):
                s = b % NG
                if b >= NG:
                    sp.wait_ge(part_done, b - NG + 1)
                sp.dma_start(x2_sb[0:LQ, s], x2_in[b]).then_inc(x2_loaded[s], 16)
                if b >= NG // 2:
                    store(b - NG // 2)
            for b in range(NB - NG // 2, NB):
                store(b)
            for s in range(NG):
                sp.wait_ge(out_stored[s], NB // NG * 16)

        @block.gpsimd
        def _(pool):
            pool.memset(ones[:, :], 1.0).then_inc(made, 1)
            pool.memset(ident2[:, :], 0.0).then_inc(made, 1)
            pool.wait_ge(made, 2)
            pool.affine_select(out=before_me[:, :], in_=ones[:, :], compare_op=ALU.is_gt, fill=0.0, base=0,
                               pattern=[[1, 128]], channel_multiplier=-1).then_inc(made, 1)
            pool.affine_select(out=ident2[:, :], in_=ident2[:, :], compare_op=ALU.not_equal, fill=1.0, base=0,
                               pattern=[[-1, 128]], channel_multiplier=1).then_inc(made, 1)
            pool.iota(tile_no[:, :], pattern=[[1, TILES]], base=0, channel_multiplier=0,
                      allow_small_or_imprecise_dtypes=True).then_inc(made, 1)
            pool.wait_ge(slots_ready, 1)
            pool.wait_ge(xn_loaded, 64)
            for b in range(NB):
                for k in range(TOPK):
                    pool.indirect_dma_start(sorted_x, bass.IndirectOffsetOnAxis(ap=slot_i[0:LQ, k, b:b + 1], axis=0), xn_all[0:LQ, b], None).then_inc(scattered, 16)
            for s in range(2):
                pool.wait_ge(y_stored[s], (TILES + 1 - s) // 2 * 16)
            for b in range(NB):
                s = b % NG
                if b >= NG:
                    pool.wait_ge(out_ready, b - NG + 1)
                for k in range(TOPK):
                    pool.indirect_dma_start(y_in[0:LQ, s, k], None, sorted_y, bass.IndirectOffsetOnAxis(ap=slot_i[0:LQ, k, b:b + 1], axis=0)).then_inc(gathered[s], 16)

        @block.scalar
        def _(act):
            act.wait_ge(tanh_loaded, 16)
            act.activation(tanh_f[:, :], tanh_f[:, :], ACT.Tanh).then_inc(act_done, 1)
            act.wait_ge(ratio_ready, 1)
            act.activation(ratio[0:LQ, 1], ratio[0:LQ, 0], ACT.Exp).then_inc(act_done, 1)

            def body(t):
                if t.has(0):
                    act.wait_ge(ht_done, t(2, 1))
                    if t.at >= 1:
                        act.wait_ge(y_done, t(1))
                    act.activation(ht_sb[:, 0:4], ht_ps[0][:, :].rearrange("p (c t) -> p c t", c=4), ACT.Copy).then_inc(ht_copied[0], 1)
                if t.has(1):
                    for n in range(2):
                        act.wait_ge(biased, t(2, 2 + n + 1))
                        if t.at >= 0:
                            act.wait_ge(ht_done, t(2, 2))
                        act.activation(g_sb[:, n], h_sb[:, n], ACT.Gelu).then_inc(gelu_done, 1)

            tiles(act, body)

        @block.vector
        def _(dve):
            n_step = [0]

            def then(instruction):
                n_step[0] += 1
                instruction.then_inc(step, 1)
                dve.wait_ge(step, n_step[0])

            L = slice(0, LQ)
            then(dve.tensor_tensor(ratio[L, 0], top_v[L, :, 1], top_v[L, :, 0], ALU.subtract))
            dve.sem_inc(ratio_ready, 1)
            dve.wait_ge(act_done, 2)
            then(dve.tensor_scalar(ratio[L, 2], ratio[L, 1], 1.0, None, ALU.add))
            then(dve.reciprocal(weight[L, 0], ratio[L, 2]))
            then(dve.tensor_tensor(weight[L, 1], weight[L, 0], ratio[L, 1], ALU.mult))
            then(dve.tensor_scalar(weight[L, :, :], weight[L, :, :], tanh_f[L, :], None, ALU.mult))
            then(dve.tensor_copy(top_f[L, :, :], top_i[L, :, 0:TOPK].rearrange("p b k -> p k b")))
            for e in range(E):
                last = dve.tensor_scalar(onehot[L, e], top_f[L, :, :], float(e), None, ALU.is_equal)
            then(last)
            dve.tensor_tensor(member[L, :, :], onehot[L, :, 0], onehot[L, :, 1], ALU.add).then_inc(counted, 1)
            dve.wait_ge(counted, 2)
            flat = lambda a: a.rearrange("p e b -> p (e b)")
            then(dve.tensor_copy(flat(total[L, :, :]), count_ps[L, E * NB:2 * E * NB]))
            then(dve.tensor_reduce(count_f[L, :], total[L, :, :], AX.X, ALU.add))
            then(dve.tensor_scalar(count_i[L, 0], count_f[L, :], 127.0, None, ALU.add))
            then(dve.tensor_scalar(count_i[L, 1], count_i[L, 0], 7, None, ALU.arith_shift_right))
            then(dve.tensor_copy(tiles_f[L, :], count_i[L, 1]))
            then(dve.tensor_tensor_scan(tile_end[L, :], ones[L, 0:E], tiles_f[L, :], 0.0, ALU.mult, ALU.add))
            then(dve.tensor_tensor(slot_start[L, :], tile_end[L, :], tiles_f[L, :], ALU.subtract))
            then(dve.tensor_scalar(slot_start[L, :], slot_start[L, :], 128.0, None, ALU.mult))
            for e in range(E):
                last = dve.tensor_tensor_scan(slot[L, e], ones[L, 0:NB], total[L, e], slot_start[L, e:e + 1], ALU.mult, ALU.add)
            then(last)
            then(dve.tensor_tensor(slot[L, :, :], slot[L, :, :], total[L, :, :], ALU.subtract))
            then(dve.tensor_tensor(flat(slot[L, :, :]), flat(slot[L, :, :]), count_ps[L, 0:E * NB], ALU.add))
            for k in range(TOPK):
                last = dve.tensor_tensor(picked[L, k], slot[L, :, :], onehot[L, :, k], ALU.mult)
            then(last)
            for k in range(TOPK):
                last = dve.tensor_reduce(slot_f[L, k], picked[L, k].rearrange("p e b -> p b e"), AX.X, ALU.add)
            then(last)
            then(dve.tensor_copy(slot_i[L, :, :], slot_f[L, :, :]))
            dve.sem_inc(slots_ready, 1)
            for e in range(E - 1):
                if e == 0:
                    then(dve.tensor_scalar(tile_acc[:, 0], tile_no[:, :], tile_end[0:1, 0:1], None, ALU.is_ge))
                else:
                    then(dve.scalar_tensor_tensor(out=tile_acc[:, e % 2], in0=tile_no[:, :], scalar=tile_end[0:1, e:e + 1], in1=tile_acc[:, (e - 1) % 2],
                                                  op0=ALU.is_ge, op1=ALU.add))
            then(dve.tensor_copy(tile_expert[:, :], tile_acc[:, (E - 2) % 2]))
            dve.sem_inc(slots_ready, 1)
            dve.wait_ge(weights_loaded, 16 * (2 * E + 2))

            def expert(t, offset):
                return dve.value_load(tile_expert[0:1, bass.ds(t(1, offset), 1)] if t.i is not None else tile_expert[0:1, t.at + offset:t.at + offset + 1], min_val=0, max_val=E - 1)

            def body(t):
                if t.has(0):
                    dve.wait_ge(ht_done, t(2, 2))
                    if t.at >= 1:
                        dve.wait_ge(y_done, t(1))
                    dve.tensor_copy(ht_sb[:, 4:8], ht_ps[1][:, :].rearrange("p (c t) -> p c t", c=4)).then_inc(ht_copied[1], 1)
                if t.has(1):
                    e1 = expert(t, 1)
                    for n in range(2):
                        dve.wait_ge(h_done, t(2, 2 + n + 1))
                        if t.at >= 0:
                            dve.wait_ge(gelu_done, t(2, n + 1))
                        dve.tensor_tensor(h_sb[:, n], h_ps[n][:, :], b1_sb[:, bass.ds(e1, 1), n * 512:n * 512 + 512].rearrange("p o f -> p (o f)"), ALU.add).then_inc(biased, 1)
                if t.has(2):
                    dve.wait_ge(xt_done, t(1, 3))
                    dve.tensor_copy(xt_sb[:, t.at % 2], xt_ps[:, 0:KD * 128].rearrange("p (k t) -> p k t", k=KD)).then_inc(xt_copied, 1)
                if t.has(0):
                    e0 = expert(t, 0)
                    dve.wait_ge(y_done, t(1, 1))
                    if t.at >= 2:
                        dve.wait_ge(y_stored[t.at % 2], t.halves(16, -2))
                    dve.tensor_tensor(y_sb[:, t.at % 2], y_ps[:, 0:D], b2_sb[:, bass.ds(e0, 1), :].rearrange("p o d -> p (o d)"), ALU.add).then_inc(y_ready, 1)

            tiles(dve, body)
            for b in range(NB):
                s = b % NG
                dve.wait_ge(gathered[s], (b // NG + 1) * 32)
                dve.wait_ge(x2_loaded[s], (b // NG + 1) * 16)
                dve.scalar_tensor_tensor(out=part_sb[L, s], in0=y_in[L, s, 0], scalar=weight[L, 0, b:b + 1], in1=x2_sb[L, s], op0=ALU.mult, op1=ALU.add).then_inc(part_done, 1)
                dve.wait_ge(part_done, b + 1)
                if b >= NG:
                    dve.wait_ge(out_stored[s], b // NG * 16)
                dve.scalar_tensor_tensor(out=o_sb[L, s], in0=y_in[L, s, 1], scalar=weight[L, 1, b:b + 1], in1=part_sb[L, s], op0=ALU.mult, op1=ALU.add).then_inc(out_ready, 1)

        @block.tensor
        def _(pe):
            pe.wait_ge(made, 5)
            pe.wait_ge(counted, 1)
            rows = member[0:LQ, :, :].rearrange("p e b -> p (e b)")
            nc.tensor.matmul(count_ps[0:LQ, 0:E * NB], before_me[0:LQ, 0:LQ], rows, start=True, stop=True)
            nc.tensor.matmul(count_ps[0:LQ, E * NB:2 * E * NB], ones[0:LQ, 0:LQ], rows, start=True, stop=True).then_inc(counted, 1)
            pe.wait_ge(slots_ready, 2)
            pe.wait_ge(weights_loaded, 16 * (2 * E + 1))

            def body(t):
                if t.has(1):
                    e1 = pe.value_load(tile_expert[0:1, bass.ds(t(1, 1), 1)] if t.i is not None else tile_expert[0:1, t.at + 1:t.at + 2], min_val=0, max_val=E - 1)
                for n in range(2):
                    if t.has(1):
                        if n == 0:
                            pe.wait_ge(xt_copied, t(1, 2))
                        if t.at >= 0:
                            pe.wait_ge(biased, t(2, n + 1))
                        for k in range(KD):
                            last = nc.tensor.matmul(h_ps[n][:, :], xt_sb[:, (t.at + 1) % 2, k],
                                                    w1_sb[:, k, bass.ds(e1, 1), n * 512:n * 512 + 512].rearrange("p o f -> p (o f)"), start=(k == 0), stop=(k == KD - 1))
                        last.then_inc(h_done, 1)
                    if n == 0 and t.has(0):
                        for m in range(2):
                            pe.wait_ge(gelu_done, t(2, m + 1))
                            if t.at >= 1:
                                pe.wait_ge(ht_copied[m], t(1))
                            for c in range(4):
                                last = nc.tensor.transpose(ht_ps[m][:, c * 128:c * 128 + 128], g_sb[:, m, c * 128:c * 128 + 128], ident2[:, :])
                            last.then_inc(ht_done, 1)
                if t.has(2):
                    pe.wait_ge(x_loaded[t.at % 2], t.halves(16, 2))
                    if t.at >= -1:
                        pe.wait_ge(xt_copied, t(1, 2))
                    for k in range(KD):
                        last = nc.tensor.transpose(xt_ps[:, k * 128:k * 128 + 128], x_sb[:, t.at % 2, k * 128:k * 128 + 128], ident2[:, :])
                    last.then_inc(xt_done, 1)
                if t.has(0):
                    e0 = pe.value_load(tile_expert[0:1, bass.ds(t(1), 1)] if t.i is not None else tile_expert[0:1, t.at:t.at + 1], min_val=0, max_val=E - 1)
                    for m in range(2):
                        pe.wait_ge(ht_copied[m], t(1, 1))
                    if t.at >= 1:
                        pe.wait_ge(y_ready, t(1))
                    for c in range(KF):
                        last = nc.tensor.matmul(y_ps[:, 0:D], ht_sb[:, c], w2_sb[:, c, bass.ds(e0, 1), :].rearrange("p o d -> p (o d)"), start=(c == 0), stop=(c == KF - 1))
                    last.then_inc(y_done, 1)

            tiles(pe, body)


def program(nc, x, ctx, g_x, g_f, ln_m_g, ln_m_b, ln_l_g, ln_l_b, wq, wkv, wout, gate_w, w1, b1, w2, b2, out):
    dram = lambda name, shape: nc.dram_tensor(name, shape, F32).ap()
    x2_dram = dram("x2_dram", [NB, LQ, D])
    xn_dram = dram("xn_dram", [NB, LQ, D])
    sorted_x = dram("sorted_x", [TILES * 128, D])
    sorted_y = dram("sorted_y", [TILES * 128, D])
    with ExitStack() as st:
        top_v = st.enter_context(nc.sbuf_tensor("top_v", [128, NB, TOPK], F32))
        top_i = st.enter_context(nc.sbuf_tensor("top_i", [128, NB, TOPK], U32))
        with ExitStack() as inner:
            ident = inner.enter_context(nc.sbuf_tensor("ident", [128, 128], F32))
            attention(nc, x, ctx, g_x, ln_m_g, ln_m_b, ln_l_g, ln_l_b, wq, wkv, wout, gate_w, x2_dram, xn_dram, top_v, top_i, ident, sorted_x)
        routed_ffn(nc, g_f, w1, b1, w2, b2, x2_dram, xn_dram, out, sorted_x, sorted_y, top_v, top_i)


_INS = ['x', 'ctx_1024', 'g_xattn', 'g_ffn', 'L0_xattn_ln_m_g', 'L0_xattn_ln_m_b', 'L0_xattn_ln_l_g', 'L0_xattn_ln_l_b',
        'L0_xattn_Wq', 'L0_xattn_Wkv', 'L0_xattn_Wout', 'L0_ffn_gate_w', 'L0_ffn_w1', 'L0_ffn_b1', 'L0_ffn_w2', 'L0_ffn_b2']
_OUTS = [((NB, LQ, D), 'float32')]


def kernel(**inputs):
    import numpy as _np
    import concourse.bacc as _bacc
    from concourse import mybir as _mybir
    from concourse.bass_utils import run_bass_kernel_spmd as _run

    nc = _bacc.Bacc("TRN2", target_bir_lowering=False, num_devices=1)
    arrays, args = {}, []
    for name in _INS:
        a = _np.ascontiguousarray(inputs[name])
        arrays[f"in_{name}_dram"] = a
        args.append(nc.dram_tensor(f"in_{name}_dram", a.shape, _mybir.dt.from_np(a.dtype), kind="ExternalInput").ap())
    for i, (shape, dtype) in enumerate(_OUTS):
        dt = _mybir.dt.from_np(_np.dtype(dtype))
        args.append(nc.dram_tensor(f"out_{i}_dram", shape, dt, kind="ExternalOutput").ap())
    program(nc, *args)
    r = _run(nc, [arrays], core_ids=[0])
    got = tuple(r.results[0][f"out_{i}_dram"] for i in range(len(_OUTS)))
    return got[0]
```

```python
import concourse.bass as bass
from concourse import mybir
from contextlib import ExitStack

F32 = mybir.dt.float32
F32R = mybir.dt.float32r
F16 = mybir.dt.float16
I32 = mybir.dt.int32
U32 = mybir.dt.uint32
ALU = mybir.AluOpType
ACT = mybir.ActivationFunctionType
AX = mybir.AxisListType

NB, LQ, LC, D = 32, 112, 375, 256
H, DH = 16, 64
LK = LC + LQ
LKP = LK + LK % 2
KD = D // 128
CT, CP = 3, LC // 3
NP = H // 2
KT = 4
INNER = H * DH
E, TOPK, F = 8, 2, 1024
EPS = 1e-5
ROWS = 256
TILES = (NB * LQ * TOPK + E * (ROWS - 1)) // ROWS
X_SCALE = 1024.0
UNITS = 20


class Batch:

    def __init__(self, at, i=None, step=0):
        self.at, self.i, self.step = at, i, step

    def __call__(self, per, extra=0):
        fixed = self.at * per + extra
        return fixed if self.i is None else self.i * (self.step * per) + fixed

    def has(self, offset):
        return self.i is not None or 0 <= self.at + offset < NB

    def halves(self, offset, per):
        fixed = per * ((self.at + offset) // 2 + 1)
        return fixed if self.i is None else self.i * (self.step // 2 * per) + fixed

    def parity(self, offset):
        return (self.at + offset) % 2


def batches(engine, body):
    for b in range(-2, 3):
        body(Batch(b))
    with engine.Fori(0, (NB - 6) // 2) as i:
        body(Batch(3, i, 2))
        body(Batch(4, i, 2))
    for b in range(NB - 3, NB + 1):
        body(Batch(b))


def units_of(b):
    if b.i is None and not -2 <= b.at <= NB:
        return []
    found = []
    kq, v = 0, 0
    for j in range(NP):
        if b.has(1):
            found.append(("K", j, b(10, 10 + kq + 1)))
            kq += 1
            found.append(("V", j, b(8, 8 + v + 1)))
            v += 1
        if b.has(2) and j in (4, 6):
            found.append(("T", (j - 4) // 2, b(2, 4 + (j - 4) // 2 + 1)))
        if b.has(1) and j in (5, 7):
            found.append(("Q", (j - 5) // 2, b(10, 10 + kq + 1)))
            kq += 1
    return found


def first_unit(b):
    if b.i is None and b.at == -2:
        return 0
    return b(UNITS, 2 + UNITS)


def before(b):
    return Batch(b.at - 1, b.i, b.step)


def lag_batch(b):
    return b.i is not None or b.at >= 1


def prev_pair(b, j):
    return b.has(0) if j >= 1 else lag_batch(b)


def pv_pair(b, j):
    return b.has(0) if j >= 2 else lag_batch(b)


def o_pair(b, j):
    return b.has(0) if j >= 3 else lag_batch(b)


def unit_number(b, kind, index):
    n = [u[:2] for u in units_of(b)].index((kind, index))
    return first_unit(b) + n + 1, (n + first_unit(Batch(0))) % 2


def attention(nc, x, ctx_in, g_x, ln_m_g, ln_m_b, ln_l_g, ln_l_b, wq, wkv, wout, gate_w, x2_out, xn_out, top_v, top_i, ident, w1, w2, peaks):
    with ExitStack() as st:
        sb = lambda name, shape, dt=F32: st.enter_context(nc.sbuf_tensor(name, shape, dt))
        sem = lambda name: st.enter_context(nc.semaphore(name))
        bank = lambda name: st.enter_context(nc.psum_tensor(name, [128, 512], F32))

        wkv_hi = sb("wkv_hi", [128, KD, 2 * INNER], F32R)
        wkv_lo = sb("wkv_lo", [128, KD, 2 * INNER], F32R)
        wq_sb = sb("wq_sb", [128, KD, INNER])
        wout_hi = sb("wout_hi", [128, NP, D], F32R)
        wout_lo = sb("wout_lo", [128, NP, D], F32R)
        gate_sb = sb("gate_sb", [128, KD, E])
        affine = sb("affine", [128, 4, KD])
        tanh_g = sb("tanh_g", [128, 1])
        ctx_sb = sb("ctx_sb", [128, 2, CT, D])
        x_sb = sb("x_sb", [128, 2, D])
        norm_sb = sb("norm_sb", [128, CT + 1, D])
        stats = sb("stats", [128, CT + 1, 6])
        moments = sb("moments", [128, CT + 1, 2])
        rstd = sb("rstd", [128, 4 * (CT + 1)])
        half = sb("half", [128, CT + 1])
        eps = sb("eps", [128, CT + 1])
        kv_f = sb("kv_f", [128, KD, LKP])
        lat_f = sb("lat_f", [128, 2, KD, LQ])
        kv_hi = sb("kv_hi", [128, 2, KD, LKP], F32R)
        kv_lo = sb("kv_lo", [128, 2, KD, LKP], F32R)
        q_hi = sb("q_hi", [128, H, LQ], F32R)
        q_lo = sb("q_lo", [128, H, LQ], F32R)
        k_both = sb("k_both", [128, H, LKP], F32R)
        v_sb = sb("v_sb", [128, 2, KT, INNER])
        p_sb = sb("p_sb", [128, 2, 2, 512])
        pt_sb = sb("pt_sb", [128, 2, 2, KT, LQ])
        neg_max = sb("neg_max", [128, 2, 2])
        row_sum = sb("row_sum", [128, 2, 2])
        inv_sum = sb("inv_sum", [128, 2, 2])
        o_hi = sb("o_hi", [128, 2, NP, LQ], F32R)
        o_lo = sb("o_lo", [128, 2, NP, LQ], F32R)
        res_sb = sb("res_sb", [128, 2, D])
        x2_sb = sb("x2_sb", [128, 2, D])
        xn_sb = sb("xn_sb", [128, 2, D])
        stats2 = sb("stats2", [128, 6])
        moments2 = sb("moments2", [128, 2])
        rstd2 = sb("rstd2", [128, 2])
        xnt_sb = sb("xnt_sb", [128, KD, LQ])
        logits_sb = sb("logits_sb", [128, E])
        max_v = sb("max_v", [128, 8])
        max_i = sb("max_i", [128, 8], U32)
        w_part = sb("w_part", [128, 2, 512])

        scores_ps = [bank("scores_ps0"), bank("scores_ps1")]
        pt_ps = [bank("pt_ps0"), bank("pt_ps1")]
        proj_ps = [bank("proj_ps0"), bank("proj_ps1")]
        pv_ps = bank("pv_ps")
        tail_ps = bank("tail_ps")

        w_loaded = sem("w_loaded"); small_loaded = sem("small_loaded")
        part_loaded = sem("part_loaded"); peak_done = sem("peak_done")
        w_hi_done = sem("w_hi_done"); w_ready = sem("w_ready"); set_up = sem("set_up"); tanh_done = sem("tanh_done")
        ctx_loaded = [sem("ctx_loaded0"), sem("ctx_loaded1")]
        res_loaded = [sem("res_loaded0"), sem("res_loaded1")]
        stats_done = sem("stats_done"); moments_done = sem("moments_done"); pool_step = sem("pool_step")
        norm_done = sem("norm_done")
        proj_done = sem("proj_done"); kq_hi = sem("kq_hi"); q_copied = sem("q_copied"); kq_lo = sem("kq_lo"); v_copied = sem("v_copied")
        kv_affine = sem("kv_affine"); kvhi_done = sem("kvhi_done"); kvlo_done = sem("kvlo_done")
        scores_done = sem("scores_done"); max_done = sem("max_done"); exp_done = sem("exp_done"); inv_done = sem("inv_done"); p_ready = sem("p_ready")
        pt_done = sem("pt_done"); pt_copied = [sem("pt_copied_act"), sem("pt_copied_dve")]
        pv_done = sem("pv_done"); o_high = sem("o_high"); o_copied = sem("o_copied")
        out_done = sem("out_done"); x2_done = sem("x2_done"); stats2_done = sem("stats2_done"); rstd2_done = sem("rstd2_done")
        xn_done = sem("xn_done"); xnt_done = sem("xnt_done"); xnt_copied = sem("xnt_copied"); logits_done = sem("logits_done")
        logits_copied = sem("logits_copied"); top_done = sem("top_done"); stored = [sem("stored0"), sem("stored1")]

        block = st.enter_context(nc.Block())

        v_flat = v_sb[:, :, :, :].rearrange("p a b c -> p (a b c)")
        stage = v_flat[:, 0:KD * 2 * INNER].rearrange("p (k n) -> p k n", k=KD)
        stage_out = v_flat[:, KD * 2 * INNER:KD * 2 * INNER + NP * D].rearrange("p (j n) -> p j n", j=NP)

        @block.sync
        def _(sp):
            def load(b, off):
                s = b.parity(off)
                c = b(1, off)
                cx = ctx_in[c] if isinstance(c, int) else ctx_in[bass.ds(c, 1)].rearrange("o n d -> (o n) d")
                xx = x[c] if isinstance(c, int) else x[bass.ds(c, 1)].rearrange("o n d -> (o n) d")
                sp.dma_start(ctx_sb[0:CP, s], cx.rearrange("(t p) d -> p t d", p=CP)).then_inc(ctx_loaded[s], 16)
                sp.dma_start(x_sb[0:LQ, s], xx).then_inc(ctx_loaded[s], 16)

            load(Batch(0), 0)
            for k in range(KD):
                sp.dma_start(stage[:, k], wkv[k * 128:(k + 1) * 128]).then_inc(w_loaded, 16)
            for n, a in enumerate((ln_m_g, ln_m_b, ln_l_g, ln_l_b)):
                sp.dma_start(affine[:, n, :], a.rearrange("(k p) -> p k", p=128), allow_slow_non_contiguous=True).then_inc(small_loaded, 16)
            sp.dma_start(tanh_g[:, :], g_x.partition_broadcast(128)).then_inc(small_loaded, 16)
            sp.dma_start(gate_sb[:, :, :], gate_w.rearrange("(k p) e -> p k e", p=128)).then_inc(small_loaded, 16)
            load(Batch(0), 1)
            sp.dma_start(wq_sb[:, :, :], wq.rearrange("(k p) n -> p k n", p=128)).then_inc(small_loaded, 16)
            sp.dma_start(stage_out, wout.rearrange("(j p) n -> p j n", p=128)).then_inc(small_loaded, 16)

            def body(b):
                if b.has(3) and not (b.i is None and b.at < -1):
                    sp.wait_ge(norm_done, b(1, 2))
                    load(b, 3)
                if b.has(0):
                    if lag_batch(b):
                        sp.wait_ge(peak_done, b(1))
                    for n, w in enumerate((w1, w2)):
                        rows = w.rearrange("e a b -> (e a) b")
                        each = rows.shape[0] // NB
                        part = rows[b.at * each:(b.at + 1) * each] if b.i is None else rows[bass.ds(b(each), each)]
                        part = part.rearrange("r (a n) -> (r a) n", n=512) if n == 0 else part.rearrange("(r a) n -> r (a n)", a=2)
                        sp.dma_start(w_part[:, n], part).then_inc(part_loaded, 16)
                    s = b.parity(0)
                    if b.at >= 2:
                        sp.wait_ge(x2_done, b(1, -1))
                    c = b(1)
                    xx = x[c] if isinstance(c, int) else x[bass.ds(c, 1)].rearrange("o n d -> (o n) d")
                    sp.dma_start(res_sb[0:LQ, s], xx).then_inc(res_loaded[s], 16)
                if b.has(-1) and not (b.i is None and b.at < 1):
                    s = b.parity(-1)
                    c = b(1, -1)
                    o1, o2 = (t[c] if isinstance(c, int) else t[bass.ds(c, 1)].rearrange("o n d -> (o n) d") for t in (x2_out, xn_out))
                    sp.wait_ge(x2_done, b(1))
                    sp.dma_start(o1, x2_sb[0:LQ, s]).then_inc(stored[s], 16)
                    sp.wait_ge(xn_done, b(1))
                    sp.dma_start(o2, xn_sb[0:LQ, s]).then_inc(stored[s], 16)

            batches(sp, body)
            for s in stored:
                sp.wait_ge(s, NB // 2 * 32)

        @block.gpsimd
        def _(pool):
            pool.memset(ident[:, :], 0.0).then_inc(pool_step, 1)
            pool.memset(half[:, :], -0.5).then_inc(pool_step, 1)
            pool.wait_ge(pool_step, 2)
            pool.affine_select(out=ident[:, :], in_=ident[:, :], compare_op=ALU.not_equal, fill=1.0, base=0,
                               pattern=[[-1, 128]], channel_multiplier=1).then_inc(pool_step, 1)
            pool.memset(kv_f[:, :, LK:LKP], 0.0).then_inc(pool_step, 1)
            for s in range(2):
                for h in range(2):
                    pool.memset(p_sb[0:LQ, s, h, LK:512], 0.0).then_inc(pool_step, 1)
            pool.memset(moments[:, :, :], 1.0).then_inc(pool_step, 1)
            pool.memset(eps[:, :], EPS).then_inc(pool_step, 1)
            pool.wait_ge(pool_step, 10)
            pool.sem_inc(set_up, 1)

            N = CT + 1
            r = lambda a, k=None: rstd[0:CP, a * N:(a + 1) * N] if k is None else rstd[0:LQ, a * N + CT:a * N + CT + 1]
            COUNT = 8

            def normalise(b, op, done):
                s = b.parity(2)
                rows_c = ctx_sb[0:CP, s] if op == ALU.subtract else norm_sb[0:CP, 0:CT]
                rows_l = x_sb[0:LQ, s] if op == ALU.subtract else norm_sb[0:LQ, CT]
                if op == ALU.subtract:
                    col_c, col_l = moments[0:CP, 0:CT, 0:1], moments[0:LQ, CT, 0:1]
                else:
                    col_c, col_l = rstd[0:CP, CT + 1:2 * CT + 1][:, :, None], rstd[0:LQ, 2 * CT + 1:2 * CT + 2]
                pool.tensor_tensor(norm_sb[0:CP, 0:CT], rows_c, col_c.broadcast_to((CP, CT, D)), op)
                pool.tensor_tensor(norm_sb[0:LQ, CT], rows_l, col_l.broadcast_to((LQ, D)), op).then_inc(done, 1)

            def body(b):
                step = lambda n: b(COUNT, 2 * COUNT + 10 + n)
                s = b.parity(2)
                for j in range(NP):
                    if b.has(0):
                        for h in range(2):
                            pool.wait_ge(inv_done, b(H, 2 * j + h + 1))
                            p = p_sb[0:LQ, j % 2, h, 0:LK]
                            pool.tensor_tensor(p, p, inv_sum[0:LQ, j % 2, h:h + 1].broadcast_to((LQ, LK)), ALU.mult).then_inc(p_ready, 1)
                    if b.has(2) and j == 1:
                        pool.wait_ge(moments_done, b(1, 3))
                        pool.tensor_tensor(r(0), moments[0:CP, :, 1], eps[0:CP, :], ALU.add).then_inc(pool_step, 1)
                        pool.wait_ge(pool_step, step(1))
                        pool.tensor_tensor(r(1), r(0), half[0:CP, :], ALU.pow).then_inc(pool_step, 1)
                        pool.wait_ge(pool_step, step(2))
                        pool.tensor_tensor(r(2, 1), r(1, 1), r(1, 1), ALU.mult).then_inc(pool_step, 1)
                        pool.wait_ge(pool_step, step(3))
                        pool.tensor_tensor(r(3, 1), r(2, 1), moments[0:LQ, CT:CT + 1, 1], ALU.mult).then_inc(pool_step, 1)
                        pool.wait_ge(pool_step, step(4))
                        pool.tensor_tensor(r(2, 1), r(3, 1), eps[0:LQ, 0:1], ALU.add).then_inc(pool_step, 1)
                        pool.wait_ge(pool_step, step(5))
                        pool.tensor_tensor(r(3, 1), r(2, 1), half[0:LQ, 0:1], ALU.pow).then_inc(pool_step, 1)
                        pool.wait_ge(pool_step, step(6))
                        pool.tensor_tensor(r(1, 1), r(1, 1), r(3, 1), ALU.mult).then_inc(pool_step, 1)
                    if b.has(2) and j == 2:
                        pool.wait_ge(pool_step, step(7))
                        if b.i is not None or b.at > -2:
                            pool.wait_ge(kv_affine, b(2, 4))
                        normalise(b, ALU.subtract, pool_step)
                    if b.has(2) and j == 3:
                        pool.wait_ge(pool_step, step(8))
                        normalise(b, ALU.mult, norm_done)
                    if lag_batch(b) and j == 3:
                        pool.wait_ge(stats2_done, b(2))
                        pool.tensor_tensor(rstd2[0:LQ, 0:1], moments2[0:LQ, 1:2], eps[0:LQ, 0:1], ALU.add).then_inc(rstd2_done, 1)
                        pool.wait_ge(rstd2_done, b(2, -1))
                        pool.tensor_tensor(rstd2[0:LQ, 1:2], rstd2[0:LQ, 0:1], half[0:LQ, 0:1], ALU.pow).then_inc(rstd2_done, 1)
                    if b.has(2) and j in (5, 7):
                        k = (j - 5) // 2
                        pool.wait_ge(kvhi_done, b(2, 4 + k + 1))
                        pool.tensor_tensor(kv_lo[:, s, k], kv_f[:, k], kv_hi[:, s, k].bitcast(F32), ALU.subtract).then_inc(kvlo_done, 1)

            batches(pool, body)

        @block.scalar
        def _(act):
            act.wait_ge(small_loaded, 16 * 8)
            act.activation(tanh_g[:, :], tanh_g[:, :], ACT.Tanh).then_inc(tanh_done, 1)

            def q_high(b, j):
                done, k = unit_number(b, "Q", j)
                act.wait_ge(proj_done, done)
                for r in range(2):
                    last = act.activation(q_hi[0:64, 8 * j + r:8 * j + 8:2], proj_ps[k][64 * r:64 * r + 64, 0:4 * LQ].rearrange("p (m q) -> p m q", m=4),
                                          ACT.Copy, scale=float(DH) ** -0.5)
                last.then_inc(kq_hi, 1)

            def q_again(tensor, j):
                act.activation(tensor[64:128, 8 * j:8 * j + 8], tensor[0:64, 8 * j:8 * j + 8].bitcast(F32), ACT.Copy).then_inc(q_copied, 1)

            def body(b):
                for j in range(NP):
                    if o_pair(b, j):
                        act.wait_ge(pv_done, b(NP, j - 2))
                        act.activation(o_hi[:, b.parity(0 if j >= 3 else -1), (j - 3) % NP], pv_ps[:, 0:LQ], ACT.Copy).then_inc(o_high, 1)
                    if b.has(0) and j == 0:
                        q_high(before(b), 1)
                    if b.has(1) and j == 6:
                        q_high(b, 0)
                    if lag_batch(b) and j == 6:
                        act.wait_ge(xnt_done, b(1))
                        act.activation(xnt_sb[:, :, :], tail_ps[:, 0:KD * LQ].rearrange("p (k q) -> p k q", k=KD), ACT.Copy).then_inc(xnt_copied, 1)
                    if b.has(0):
                        for h in range(2):
                            act.wait_ge(max_done, b(H, 2 * j + h + 1))
                            act.activation(p_sb[0:LQ, j % 2, h, 0:LK], scores_ps[h][0:LQ, 0:LK], ACT.Exp,
                                           bias=neg_max[0:LQ, j % 2, h:h + 1], accum_out=row_sum[0:LQ, j % 2, h:h + 1]).then_inc(exp_done, 1)
                    if b.has(1):
                        done, k = unit_number(b, "K", j)
                        act.wait_ge(proj_done, done)
                        for r in range(2):
                            last = act.activation(k_both[0:64, 2 * j + r], proj_ps[k][64 * r:64 * r + 64, 0:LKP], ACT.Copy)
                        last.then_inc(kq_hi, 1)
                    if prev_pair(b, j):
                        act.wait_ge(pt_done, b(H, 2 * j - 1))
                        act.activation(pt_sb[:, (j - 1) % 2, 0], pt_ps[0][:, 0:KT * LQ].rearrange("p (t q) -> p t q", t=KT), ACT.Copy).then_inc(pt_copied[0], 1)
                    if b.has(2) and j in (5, 7):
                        k = (j - 5) // 2
                        act.wait_ge(kv_affine, b(2, 4 + k + 1))
                        act.activation(kv_hi[:, b.parity(2), k], kv_f[:, k], ACT.Copy).then_inc(kvhi_done, 1)
                    if b.has(1):
                        done, k = unit_number(b, "V", j)
                        act.wait_ge(proj_done, done)
                        t, half_ = j % KT, j // KT
                        rows = 128 if t < KT - 1 else LKP - 128 * (KT - 1)
                        if b.i is None and b.at in (-1, 0) and j == 0:
                            act.wait_ge(w_ready, b.at + 2)
                        act.activation(v_sb[0:rows, b.parity(1), t, half_ * 512:half_ * 512 + 512], proj_ps[k][0:rows, :], ACT.Copy).then_inc(v_copied, 1)
                    if b.has(1) and j == 6:
                        act.wait_ge(kq_hi, b(10, 10 + 7))
                        q_again(q_hi, 0)
                    if b.has(1) and j == 7:
                        act.wait_ge(kq_lo, b(10, 10 + 7))
                        q_again(q_lo, 0)
                    if b.has(0) and j == 0:
                        act.wait_ge(kq_hi, b(10, 10))
                        q_again(q_hi, 1)
                    if b.has(0) and j == 1:
                        act.wait_ge(kq_lo, b(10, 10))
                        q_again(q_lo, 1)

            batches(act, body)

        @block.vector
        def _(dve):
            dve.wait_ge(set_up, 1)

            def split_wkv():
                for k in range(KD):
                    dve.wait_ge(w_loaded, 32)
                    dve.tensor_copy(wkv_hi[:, k], stage[:, k]).then_inc(w_hi_done, 1)
                for k in range(KD):
                    dve.wait_ge(w_hi_done, k + 1)
                    dve.tensor_tensor(wkv_lo[:, k], stage[:, k], wkv_hi[:, k].bitcast(F32), ALU.subtract).then_inc(w_hi_done, 1)
                dve.wait_ge(w_hi_done, 4)
                dve.memset(v_sb[96:128, 0, KT - 1], 0.0).then_inc(w_ready, 1)

            def split_wout():
                dve.tensor_copy(wout_hi[:, :, :], stage_out).then_inc(w_hi_done, 1)
                dve.wait_ge(w_hi_done, 5)
                dve.tensor_tensor(wout_lo[:, :, :], stage_out, wout_hi[:, :, :].bitcast(F32), ALU.subtract).then_inc(w_hi_done, 1)
                dve.wait_ge(w_hi_done, 6)
                dve.memset(v_sb[96:128, 1, KT - 1], 0.0).then_inc(w_ready, 1)

            def q_low(b, j):
                dve.wait_ge(kq_hi, b(10, 10 + (7 if j == 0 else 10)))
                k = unit_number(b, "Q", j)[1]
                for r in range(2):
                    last = dve.scalar_tensor_tensor(out=q_lo[0:64, 8 * j + r:8 * j + 8:2], in0=proj_ps[k][64 * r:64 * r + 64, 0:4 * LQ].rearrange("p (m q) -> p m q", m=4),
                                                    scalar=float(DH) ** -0.5, in1=q_hi[0:64, 8 * j + r:8 * j + 8:2].bitcast(F32), op0=ALU.mult, op1=ALU.subtract)
                last.then_inc(kq_lo, 1)

            def body(b):
                s = b.parity(2)
                sl = b.parity(-1)
                for j in range(NP):
                    if b.i is None and b.at == -2 and j == 2:
                        split_wkv()
                        dve.wait_ge(small_loaded, 16 * 8)
                    if b.i is None and b.at == -1 and j == 6:
                        split_wout()
                        dve.wait_ge(tanh_done, 1)
                    if lag_batch(b) and j == 3:
                        dve.wait_ge(out_done, b(1))
                        dve.wait_ge(res_loaded[sl], b.halves(-1, 16))
                        if b.i is not None or b.at >= 3:
                            dve.wait_ge(stored[sl], b.halves(-3, 32))
                        dve.scalar_tensor_tensor(out=x2_sb[0:LQ, sl], in0=tail_ps[0:LQ, 0:D], scalar=tanh_g[0:LQ, 0:1], in1=res_sb[0:LQ, sl],
                                                 op0=ALU.mult, op1=ALU.add).then_inc(x2_done, 1)
                        dve.wait_ge(x2_done, b(1))
                        dve.bn_stats(stats2[0:LQ, :], x2_sb[0:LQ, sl]).then_inc(stats2_done, 1)
                    if lag_batch(b) and j == 7:
                        dve.wait_ge(logits_done, b(1))
                        dve.tensor_copy(logits_sb[0:LQ, :], tail_ps[0:LQ, 256:256 + E]).then_inc(logits_copied, 1)
                    if b.has(2) and j == 1:
                        dve.wait_ge(stats_done, b(CT + 1, 3 * (CT + 1)))
                    if lag_batch(b) and j == 3:
                        dve.wait_ge(stats2_done, b(2, -1))
                    if lag_batch(b) and j == 7:
                        dve.wait_ge(logits_copied, b(1))
                    if b.has(0):
                        for h in range(2):
                            dve.wait_ge(scores_done, b(H, 2 * j + h + 1))
                            dve.tensor_reduce(neg_max[0:LQ, j % 2, h:h + 1], scores_ps[h][0:LQ, 0:LK], AX.X, ALU.max, negate=True).then_inc(max_done, 1)
                    if b.has(2) and j == 1:
                        for t in range(CT + 1):
                            n = CP if t < CT else LQ
                            last = dve.bn_aggr(moments[0:n, t], stats[0:n, t])
                        last.then_inc(moments_done, 1)
                    if lag_batch(b) and j == 3:
                        dve.bn_aggr(moments2[0:LQ, :], stats2[0:LQ, :]).then_inc(stats2_done, 1)
                    if lag_batch(b) and j == 7:
                        dve.max(max_v[0:LQ, :], logits_sb[0:LQ, :]).then_inc(top_done, 1)
                    if o_pair(b, j):
                        dve.wait_ge(o_high, b(NP, j - 2))
                        dve.tensor_tensor(o_lo[:, b.parity(0 if j >= 3 else -1), (j - 3) % NP], pv_ps[:, 0:LQ],
                                          o_hi[:, b.parity(0 if j >= 3 else -1), (j - 3) % NP].bitcast(F32), ALU.subtract).then_inc(o_copied, 1)
                    if b.has(0) and j == 0:
                        q_low(before(b), 1)
                    if b.has(1) and j == 6:
                        q_low(b, 0)
                    if b.has(2) and j in (5, 7):
                        k = (j - 5) // 2
                        done, n = unit_number(b, "T", k)
                        dve.wait_ge(proj_done, done)
                        if b.i is not None or b.at > -2:
                            dve.wait_ge(kvlo_done, b(2, 2 + k + 1))
                        dve.tensor_scalar(kv_f[:, k, 0:LC], proj_ps[n][:, 0:LC], affine[:, 0, k:k + 1], affine[:, 1, k:k + 1], ALU.mult, ALU.add)
                        dve.tensor_scalar(kv_f[:, k, LC:LK], proj_ps[n][:, LC:LK], affine[:, 2, k:k + 1], affine[:, 3, k:k + 1], ALU.mult, ALU.add)
                        dve.tensor_scalar(lat_f[:, s, k], proj_ps[n][:, LC:LK], affine[:, 2, k:k + 1], affine[:, 3, k:k + 1], ALU.mult, ALU.add).then_inc(kv_affine, 1)
                    if lag_batch(b) and j == 7:
                        dve.wait_ge(top_done, b(2, -1))
                    if b.has(0):
                        for h in range(2):
                            dve.wait_ge(exp_done, b(H, 2 * j + h + 1))
                            dve.reciprocal(inv_sum[0:LQ, j % 2, h:h + 1], row_sum[0:LQ, j % 2, h:h + 1]).then_inc(inv_done, 1)
                    if lag_batch(b) and j == 7:
                        dve.max_index(max_i[0:LQ, :], max_v[0:LQ, :], logits_sb[0:LQ, :]).then_inc(top_done, 1)
                        dve.wait_ge(top_done, b(2))
                    if prev_pair(b, j):
                        dve.wait_ge(pt_done, b(H, 2 * j))
                        dve.tensor_copy(pt_sb[:, (j - 1) % 2, 1], pt_ps[1][:, 0:KT * LQ].rearrange("p (t q) -> p t q", t=KT)).then_inc(pt_copied[1], 1)
                    if b.has(1):
                        idx = 10 + (j + 1 if j < 6 else j + 2)
                        dve.wait_ge(kq_hi, b(10, idx))
                        k = unit_number(b, "K", j)[1]
                        for r in range(2):
                            last = dve.tensor_tensor(k_both[64:128, 2 * j + r], proj_ps[k][64 * r:64 * r + 64, 0:LKP], k_both[0:64, 2 * j + r].bitcast(F32), ALU.subtract)
                        last.then_inc(kq_lo, 1)
                    if b.has(2) and j == 0:
                        dve.wait_ge(ctx_loaded[s], b.halves(2, 32))
                        if b.i is not None or b.at > -2:
                            dve.wait_ge(norm_done, b(1, 2))
                        for t in range(CT + 1):
                            rows = ctx_sb[0:CP, s, t] if t < CT else x_sb[0:LQ, s]
                            dve.bn_stats(stats[0:rows.shape[0], t], rows).then_inc(stats_done, 1)
                    if b.has(0) and j == 2:
                        dve.wait_ge(part_loaded, b(32, 32))
                        c = b(1)
                        dve.tensor_reduce(peaks[:, c] if isinstance(c, int) else peaks[:, bass.ds(c, 1)].rearrange("p o w -> p (o w)"), w_part[:, :, :], AX.X, ALU.max, apply_absolute_value=True).then_inc(peak_done, 1)
                    if lag_batch(b) and j == 4:
                        dve.wait_ge(rstd2_done, b(2))
                        dve.tensor_scalar(xn_sb[0:LQ, sl], x2_sb[0:LQ, sl], moments2[0:LQ, 0:1], rstd2[0:LQ, 1:2], ALU.subtract, ALU.mult).then_inc(xn_done, 1)
                    if lag_batch(b) and j == 7:
                        c = b(1, -1)
                        to = lambda t: t[0:LQ, c] if isinstance(c, int) else t[0:LQ, bass.ds(c, 1)].rearrange("p o k -> p (o k)")
                        dve.tensor_copy(to(top_v), max_v[0:LQ, 0:TOPK])
                        dve.tensor_copy(to(top_i), max_i[0:LQ, 0:TOPK])

            batches(dve, body)

        @block.tensor
        def _(pe):
            pe.wait_ge(set_up, 1)

            def free(kind, idx):
                sem_ = {"K": kq_lo, "Q": kq_lo, "V": v_copied, "T": kv_affine}[kind]
                pe.wait_ge(sem_, idx)

            def body(b):
                units = units_of(b)
                earlier = units_of(before(b))[-2:]
                seq = earlier + units
                pos = [0]

                def take():
                    i = pos[0]
                    pos[0] += 1
                    back = i + len(earlier) - 2
                    if back >= 0:
                        free(seq[back][0], seq[back][2])
                    return proj_ps[i % 2]

                def three(out, lhs, rhs):
                    n = 0
                    for k in range(KD):
                        for a, c in ((0, 0), (0, 1), (1, 0)):
                            last = nc.tensor.matmul(out, lhs(a, k), rhs(c, k), start=(n == 0), stop=(n == 3 * KD - 1))
                            n += 1
                    return last

                for j in range(NP):
                    if b.has(0):
                        s = b.parity(0)
                        if j == 0:
                            pe.wait_ge(kq_lo, b(10, 9))
                        if j in (0, 4):
                            pe.wait_ge(q_copied, b(4, 2 if j == 0 else 4))
                        for h in range(2):
                            if j or lag_batch(b):
                                pe.wait_ge(exp_done, b(H, 2 * j + h - 1))
                            for n, part in enumerate((q_hi, q_lo)):
                                last = nc.tensor.matmul(scores_ps[h][0:LQ, 0:LKP], part[:, 2 * j + h], k_both[:, 2 * j + h], start=(n == 0), stop=(n == 1))
                            last.then_inc(scores_done, 1)
                    if b.has(1):
                        s1 = b.parity(1)
                        if j == 0:
                            pe.wait_ge(kvlo_done, b(2, 4))
                            if b.i is None and b.at == -1:
                                pe.wait_ge(w_ready, 1)
                        ps = take()
                        three(ps[:, 0:LKP], lambda a, k: (wkv_hi, wkv_lo)[a][:, k, j * 128:j * 128 + 128],
                              lambda c, k: (kv_hi, kv_lo)[c][:, s1, k]).then_inc(proj_done, 1)
                    if prev_pair(b, j):
                        for h in range(2):
                            pe.wait_ge(p_ready, b(H, 2 * j - 1 + h))
                            if j >= 2 or lag_batch(b):
                                pe.wait_ge(pt_copied[h], b(NP, j - 1))
                            for t in range(KT):
                                last = nc.tensor.transpose(pt_ps[h][:, t * LQ:(t + 1) * LQ], p_sb[0:LQ, (j - 1) % 2, h, t * 128:(t + 1) * 128], ident[0:LQ, 0:LQ])
                            last.then_inc(pt_done, 1)
                    if b.has(1):
                        t, half_ = j % KT, j // KT
                        rows = 128 if t < KT - 1 else LKP - 128 * (KT - 1)
                        ps = take()
                        three(ps[0:rows, :], lambda a, k: (kv_hi, kv_lo)[a][:, s1, k, t * 128:t * 128 + rows],
                              lambda c, k: (wkv_hi, wkv_lo)[c][:, k, INNER + half_ * 512:INNER + half_ * 512 + 512]).then_inc(proj_done, 1)
                    if pv_pair(b, j):
                        p = (j - 2) % NP
                        sv = b.parity(0 if j >= 2 else -1)
                        for h in range(2):
                            pe.wait_ge(pt_copied[h], b(NP, j - 1))
                        if j == 2:
                            pe.wait_ge(v_copied, b(8, 8))
                        if j >= 3 or lag_batch(b):
                            pe.wait_ge(o_copied, b(NP, j - 2))
                        for t in range(KT):
                            for h in range(2):
                                n = 2 * p + h
                                last = nc.tensor.matmul(pv_ps[64 * h:64 * h + 64, 0:LQ], v_sb[:, sv, t, n * DH:(n + 1) * DH], pt_sb[:, (j - 2) % 2, h, t],
                                                        start=(t == 0), stop=(t == KT - 1))
                        last.then_inc(pv_done, 1)
                    if lag_batch(b):
                        sl = b.parity(-1)
                        if j == 2:
                            if b.i is None and b.at == 1:
                                pe.wait_ge(w_ready, 2)
                            pe.wait_ge(o_copied, b(NP))
                            if b.i is not None or b.at >= 2:
                                pe.wait_ge(logits_copied, b(1, -1))
                            for p in range(NP):
                                for n, (oo, ww) in enumerate(((o_hi, wout_hi), (o_hi, wout_lo), (o_lo, wout_hi))):
                                    last = nc.tensor.matmul(tail_ps[0:LQ, 0:D], oo[:, sl, p], ww[:, p], start=(p == n == 0), stop=(p == NP - 1 and n == 2))
                            last.then_inc(out_done, 1)
                        if j == 5:
                            pe.wait_ge(xn_done, b(1))
                            for k in range(KD):
                                last = nc.tensor.transpose(tail_ps[:, k * LQ:(k + 1) * LQ], xn_sb[0:LQ, sl, k * 128:(k + 1) * 128], ident[0:LQ, 0:LQ])
                            last.then_inc(xnt_done, 1)
                        if j == 6:
                            pe.wait_ge(xnt_copied, b(1))
                            for k in range(KD):
                                last = nc.tensor.matmul(tail_ps[0:LQ, 256:256 + E], xnt_sb[:, k], gate_sb[:, k], start=(k == 0), stop=(k == KD - 1))
                            last.then_inc(logits_done, 1)
                    if b.has(2) and j in (4, 6):
                        k = (j - 4) // 2
                        if k == 0:
                            pe.wait_ge(norm_done, b(1, 3))
                        ps = take()
                        for t in range(CT):
                            nc.tensor.transpose(ps[:, t * CP:(t + 1) * CP], norm_sb[0:CP, t, k * 128:(k + 1) * 128], ident[0:CP, 0:CP])
                        nc.tensor.transpose(ps[:, LC:LK], norm_sb[0:LQ, CT, k * 128:(k + 1) * 128], ident[0:LQ, 0:LQ]).then_inc(proj_done, 1)
                    if b.has(1) and j in (5, 7):
                        ps = take()
                        for m in range(4):
                            jj = (j - 5) // 2 * 4 + m
                            for k in range(KD):
                                last = nc.tensor.matmul(ps[:, m * LQ:(m + 1) * LQ], wq_sb[:, k, jj * 128:jj * 128 + 128], lat_f[:, s1, k], start=(k == 0), stop=(k == KD - 1))
                        last.then_inc(proj_done, 1)

            batches(pe, body)

def routed_ffn(nc, g_x, w1, b1, w2, b2, x2_in, xn_in, out, y_rows, top_v, top_i, peaks):
    NTOK = NB * TOPK
    with ExitStack() as st:
        sb = lambda name, shape, dt=F32: st.enter_context(nc.sbuf_tensor(name, shape, dt))
        sem = lambda name: st.enter_context(nc.semaphore(name))
        bank = lambda name: st.enter_context(nc.psum_tensor(name, [128, 512], F32))
        KF = F // 128

        w1_hi = sb("w1_hi", [128, KD, E, F], F16)
        w1_lo = sb("w1_lo", [128, KD, E, F], F16)
        w2_hi = sb("w2_hi", [128, KF, E, D], F16)
        w2_lo = sb("w2_lo", [128, KF, E, D], F16)
        space = sb("space", [128, NB + 4, D])
        N_HALF = 2 * TILES
        halves_of = lambda a, n: a.rearrange("p s n -> p (s n)").bitcast(F16)[:, 0:NTOK * n].rearrange("p (k b n) -> p k b n", k=TOPK, n=n)
        low_hot = halves_of(space[:, 0:NTOK // 4], 128)
        high_hot = halves_of(space[:, NTOK // 4:NB + 4], N_HALF)
        x_sb = space[:, 0:4].rearrange("p (s a) d -> p s a d", s=2)
        g_sb = space[:, 4:8].rearrange("p (m c) d -> p m c d", m=2)
        y_sb = space[:, 8:12].rearrange("p (s a) d -> p s a d", s=2)
        GB, NG = 2, 4
        GROUPS = NB // GB
        y_in = space[:, 0:16].rearrange("p (s k b) d -> p s k b d", s=NG, k=TOPK)
        x2_sb, o_sb = (space[:, at:at + 8].rearrange("p (s b) d -> p s b d", s=NG) for at in (16, 24))
        stage = sb("stage", [128, 2, 2048])
        g_parts = stage[:, :, :].rearrange("p s n -> p (s n)").bitcast(F16).rearrange("p (s a m c n) -> p s a m c n", s=2, a=2, m=4, c=2)
        g_hi, g_lo = g_parts[:, :, 0], g_parts[:, :, 1]
        b1_rows = sb("b1_rows", [E * KF, 128])
        b1_sb = sb("b1_sb", [128, E, KF])
        b2_sb = sb("b2_sb", [128, E, D])
        xt_hi = sb("xt_hi", [128, 2, KD, ROWS], F16)
        xt_lo = sb("xt_lo", [128, 2, KD, ROWS], F16)
        ident2 = sb("ident2", [128, 128])
        peak = sb("peak", [128, 3])
        peak_t = sb("peak_t", [3, 1])
        peak_diag = sb("peak_diag", [3, 3])
        peak_e = sb("peak_e", [128, 3])
        exponent = sb("exponent", [128, 4, 3], I32)
        scale_i = sb("scale_i", [128, 2, 3], I32)
        scale = scale_i[:, 0].bitcast(F32)
        inverse = scale_i[:, 1].bitcast(F32)
        undo = sb("undo", [128, 2])

        onehot = sb("onehot", [128, E, TOPK, NB])
        member = sb("member", [128, E, NB])
        total = sb("total", [128, E, NB])
        slot = sb("slot", [128, E, NB])
        picked = sb("picked", [128, TOPK, E, NB])
        token_f = picked[:, :, :, :].rearrange("p k e b -> p (k e b)")[:, 0:14 * TILES].rearrange("p (a s) -> p a s", a=7)
        slot_f = sb("slot_f", [128, TOPK, NB])
        slot_i = sb("slot_i", [128, TOPK, NB], I32)
        high_i = sb("high_i", [128, TOPK, NB], I32)
        high_f = sb("high_f", [128, TOPK, NB])
        low_f = sb("low_f", [128, TOPK, NB])
        columns = sb("columns", [128, 128])
        token_no = sb("token_no", [128, 2, NB // 2])
        token_i = sb("token_i", [128, 2 * TILES], I32)
        y_row_i = sb("y_row_i", [128, 2 * TILES], I32)
        spare_row = sb("spare_row", [128, 2 * TILES])
        top_f = sb("top_f", [128, TOPK, NB])
        count_f = sb("count_f", [128, E])
        count_i = sb("count_i", [128, 2, E], I32)
        tiles_f = sb("tiles_f", [128, E])
        tile_end = sb("tile_end", [128, E])
        slot_start = sb("slot_start", [128, E])
        ones = sb("ones", [128, 128])
        before_me = sb("before_me", [128, 128])
        tile_no = sb("tile_no", [1, TILES])
        tile_acc = sb("tile_acc", [1, 2, TILES])
        tile_expert = sb("tile_expert", [1, TILES], I32)
        weight = sb("weight", [128, TOPK, NB])
        ratio = sb("ratio", [128, 3, NB])
        tanh_f = sb("tanh_f", [128, 1])

        h_ps = [bank(f"h_ps{m}") for m in range(4)]
        xt_ps = bank("xt_ps")
        y_ps = [bank("y_ps0"), bank("y_ps1")]
        small_ps = bank("small_ps")

        made = sem("made"); weights_loaded = [sem(f"weights_loaded{i}") for i in range(4)]; tanh_loaded = sem("tanh_loaded")
        step = sem("step"); counted = sem("counted"); ratio_ready = sem("ratio_ready"); act_done = sem("act_done")
        slots_ready = sem("slots_ready"); highs_hot = sem("highs_hot"); highs_ready = sem("highs_ready"); lows_ready = sem("lows_ready"); tokens_counted = sem("tokens_counted"); tokens_ready = sem("tokens_ready")
        x_loaded = [sem("xs_loaded0"), sem("xs_loaded1")]
        xt_done = sem("xt_done"); xt_high = sem("xt_high"); xt_copied = sem("xt_copied"); h_done = sem("h_done"); gelu_done = sem("gelu_done")
        g_high = sem("g_high"); g_ready = sem("g_ready")
        b_loaded = sem("b_loaded"); peaks_moved = sem("peaks_moved"); scales_ready = sem("scales_ready"); w_high = sem("w_high"); w_split = sem("w_split"); w_split_pool = sem("w_split_pool")
        y_done = sem("y_done"); y_ready = sem("y_ready"); y_stored = [sem("y_stored0"), sem("y_stored1")]
        y_loaded = [sem(f"y_loaded{i}") for i in range(NG)]
        x2_loaded = [sem(f"x2_loaded{i}") for i in range(NG)]
        part_done = sem("part_done"); out_ready = sem("out_ready"); out_stored = [sem(f"out_stored{i}") for i in range(NG)]

        block = st.enter_context(nc.Block())
        xn_rows = xn_in.rearrange("b p d -> (b p) d")
        y_by_batch = y_rows[0:TOPK * NB * LQ].rearrange("(k b p) d -> p k b d", k=TOPK, p=LQ)

        class Tile:
            def __init__(self, at, i=None):
                self.at, self.i = at, i

            def __call__(self, per, extra=0):
                fixed = self.at * per + extra
                return fixed if self.i is None else self.i * (2 * per) + fixed

            def halves(self, per, offset=0):
                fixed = per * ((self.at + offset) // 2 + 1)
                return fixed if self.i is None else self.i * per + fixed

            def has(self, offset):
                return self.i is not None or 0 <= self.at + offset < TILES

        def tiles(engine, body):
            for t in range(-2, 2):
                body(Tile(t))
            n = (TILES - 4) // 2
            with engine.Fori(0, n) as i:
                body(Tile(2, i))
                body(Tile(3, i))
            for t in range(2 + 2 * n, TILES):
                body(Tile(t))

        UNIT_COUNT = 4 * E
        slots_of_stage = stage[:, :, :].rearrange("p s (h n) -> p (s h) n", h=2)

        def unit_source(u):
            e, n = u // 4, u % 2
            if u % 4 < 2:
                return w1[e, n * 128:(n + 1) * 128]
            return w2[e, n * F // 2:(n + 1) * F // 2].rearrange("(c p) d -> p c d", p=128)

        def staged(u):
            part = slots_of_stage[:, u % 4]
            return part if u % 4 < 2 else part.rearrange("p (c d) -> p c d", d=D)

        def split(u, a):
            e, n = u // 4, u % 2
            if u % 4 < 2:
                return (w1_hi, w1_lo)[a][:, n, e]
            return (w2_hi, w2_lo)[a][:, n * KF // 2:(n + 1) * KF // 2, e]

        def scale_of(u):
            kind = u % 4 // 2
            return scale[:, kind:kind + 1]

        def expert(engine, t, offset):
            at = bass.ds(t(1, offset), 1) if t.i is not None else slice(t.at + offset, t.at + offset + 1)
            return engine.value_load(tile_expert[0:1, at], min_val=0, max_val=E - 1)

        @block.sync
        def _(sp):
            sp.dma_start(tanh_f[:, :], g_x.partition_broadcast(128)).then_inc(tanh_loaded, 16)
            sp.dma_start(b1_rows[:, :], b1.rearrange("e (c p) -> (e c) p", p=128)).then_inc(b_loaded, 16)
            for u in range(UNIT_COUNT):
                if u >= 4 and u % 4 == 3:
                    sp.wait_ge(w_split_pool, u // 4)
                elif u >= 4:
                    sp.wait_ge(w_split, (u - 4) // 4 * 3 + u % 4 + 1)
                sp.dma_start(staged(u), unit_source(u)).then_inc(weights_loaded[u % 4], 16)
            sp.dma_start(b2_sb[:, :, :], b2.partition_broadcast(128)).then_inc(b_loaded, 16)

            def load_x2(g):
                sp.dma_start(x2_sb[0:LQ, g % NG], x2_in[g * GB:(g + 1) * GB].rearrange("b p d -> p b d")).then_inc(x2_loaded[g % NG], 16)

            def store(g):
                sp.wait_ge(out_ready, (g + 1) * GB)
                sp.dma_start(out[g * GB:(g + 1) * GB].rearrange("b p d -> p b d"), o_sb[0:LQ, g % NG]).then_inc(out_stored[g % NG], 16)

            sp.wait_ge(tokens_counted, 1)
            for g in range(NG):
                load_x2(g)
            for s in range(2):
                sp.wait_ge(y_stored[s], (TILES + 1 - s) // 2 * 32)
            for g in range(GROUPS):
                if g >= NG:
                    sp.wait_ge(out_ready, (g - NG + 1) * GB)
                    load_x2(g)
                for k in range(TOPK):
                    sp.dma_start(y_in[0:LQ, g % NG, k], y_by_batch[:, k, g * GB:(g + 1) * GB]).then_inc(y_loaded[g % NG], 16)
                if g >= NG // 2:
                    store(g - NG // 2)
            for g in range(GROUPS - NG // 2, GROUPS):
                store(g)
            for s in range(NG):
                sp.wait_ge(out_stored[s], GROUPS // NG * 16)

        @block.gpsimd
        def _(pool):
            pool.memset(ones[:, :], 1.0).then_inc(made, 1)
            pool.memset(ident2[:, :], 0.0).then_inc(made, 1)
            pool.wait_ge(made, 2)
            pool.affine_select(out=before_me[:, :], in_=ones[:, :], compare_op=ALU.is_gt, fill=0.0, base=0,
                               pattern=[[1, 128]], channel_multiplier=-1).then_inc(made, 1)
            pool.affine_select(out=ident2[:, :], in_=ident2[:, :], compare_op=ALU.not_equal, fill=1.0, base=0,
                               pattern=[[-1, 128]], channel_multiplier=1).then_inc(made, 1)
            pool.iota(tile_no[:, :], pattern=[[1, TILES]], base=0, channel_multiplier=0,
                      allow_small_or_imprecise_dtypes=True).then_inc(made, 1)
            pool.iota(columns[:, :], pattern=[[1, 128]], base=0, channel_multiplier=0,
                      allow_small_or_imprecise_dtypes=True).then_inc(made, 1)
            pool.iota(token_no[:, :, :], pattern=[[0, 2], [LQ, NB // 2]], base=1, channel_multiplier=1,
                      allow_small_or_imprecise_dtypes=True).then_inc(made, 1)
            pool.iota(spare_row[:, :], pattern=[[128, 2 * TILES]], base=TOPK * NB * LQ + 1, channel_multiplier=1,
                      allow_small_or_imprecise_dtypes=True).then_inc(made, 1)
            pool.wait_ge(made, 8)

            def split_low(units):
                for u in units:
                    pool.wait_ge(w_high, u + 1)
                    pool.tensor_tensor(split(u, 1), staged(u), split(u, 0), ALU.subtract).then_inc(w_split_pool, 1)

            split_low((3, 7))
            for k in range(TOPK):
                pool.wait_ge(highs_hot, k + 1)
                pool.tensor_tensor(high_hot[0:LQ, k], high_hot[0:LQ, k], token_no[0:LQ, :, :].rearrange("p h b -> p (h b)")[:, :, None].broadcast_to((LQ, NB, N_HALF)),
                                   ALU.mult).then_inc(highs_ready, 1)
                split_low((11 + 4 * k,))
            split_low(range(19, UNIT_COUNT - 8, 4))

            def gather(t):
                for a in range(2):
                    n = 2 * t + a
                    pool.indirect_dma_start(x_sb[:, t % 2, a], None, xn_rows, bass.IndirectOffsetOnAxis(ap=token_i[:, n:n + 1], axis=0)).then_inc(x_loaded[t % 2], 16)

            pool.wait_ge(tokens_ready, 1)
            gather(0)
            gather(1)
            split_low(range(UNIT_COUNT - 5, UNIT_COUNT, 4))
            for t in range(TILES + 2):
                if t + 2 < TILES:
                    pool.wait_ge(xt_done, t + 1)
                    gather(t + 2)
                if t >= 2:
                    pool.wait_ge(y_ready, t - 1)
                    for a in range(2):
                        n = 2 * (t - 2) + a
                        pool.indirect_dma_start(y_rows, bass.IndirectOffsetOnAxis(ap=y_row_i[:, n:n + 1], axis=0), y_sb[:, t % 2, a], None).then_inc(y_stored[t % 2], 16)

        @block.scalar
        def _(act):
            act.wait_ge(tanh_loaded, 16)
            act.activation(tanh_f[:, :], tanh_f[:, :], ACT.Tanh).then_inc(act_done, 1)
            act.wait_ge(ratio_ready, 1)
            act.activation(ratio[0:LQ, 1], ratio[0:LQ, 0], ACT.Exp).then_inc(act_done, 1)

            act.wait_ge(scales_ready, 1)
            for u in range(UNIT_COUNT):
                act.wait_ge(weights_loaded[u % 4], (u // 4 + 1) * 16)
                high = act.activation(split(u, 0), staged(u), ACT.Copy, scale=scale_of(u))
                if u % 4 == 3:
                    act.activation(staged(u), staged(u), ACT.Copy, scale=scale_of(u)).then_inc(w_high, 1)
                else:
                    high.then_inc(w_high, 1)

            def body(t):
                if t.has(1):
                    e1 = expert(act, t, 1)
                    for m in range(4):
                        act.wait_ge(h_done, t(4, 4 + m + 1))
                        if t.at >= 0 or m >= 2:
                            act.wait_ge(g_ready, t(4, 4 + m - 1))
                        for c in range(2):
                            last = act.activation(g_sb[:, m % 2, c], h_ps[m][:, c * ROWS:c * ROWS + ROWS], ACT.Gelu,
                                                  bias=b1_sb[:, bass.ds(e1, 1), m * 2 + c:m * 2 + c + 1].rearrange("p o c -> p (o c)"), scale=undo[:, 0:1])
                        last.then_inc(gelu_done, 1)

            tiles(act, body)

        @block.vector
        def _(dve):
            n_step = [0]

            def then(instruction):
                n_step[0] += 1
                instruction.then_inc(step, 1)
                dve.wait_ge(step, n_step[0])

            n_split = [0]

            def split_low(until):
                for u in range(n_split[0], until):
                    if u % 4 == 3:
                        continue
                    dve.wait_ge(w_high, u + 1)
                    dve.scalar_tensor_tensor(out=split(u, 1), in0=staged(u), scalar=scale_of(u), in1=split(u, 0), op0=ALU.mult, op1=ALU.subtract).then_inc(w_split, 1)
                n_split[0] = until

            L = slice(0, LQ)
            then(dve.tensor_tensor(ratio[L, 0], top_v[L, :, 1], top_v[L, :, 0], ALU.subtract))
            dve.sem_inc(ratio_ready, 1)
            dve.wait_ge(act_done, 2)
            then(dve.tensor_scalar(ratio[L, 2], ratio[L, 1], 1.0, None, ALU.add))
            then(dve.reciprocal(weight[L, 0], ratio[L, 2]))
            then(dve.tensor_tensor(weight[L, 1], weight[L, 0], ratio[L, 1], ALU.mult))
            then(dve.tensor_scalar(weight[L, :, :], weight[L, :, :], tanh_f[L, :], None, ALU.mult))
            then(dve.memset(peak[:, :], 0.0))
            dve.tensor_reduce(peak[:, 0:2], peaks[:, :, :].rearrange("p b w -> p w b"), AX.X, ALU.max)
            dve.wait_ge(b_loaded, 16)
            then(dve.tensor_reduce(peak[0:E * KF, 2:3], b1_rows[:, :], AX.X, ALU.max, apply_absolute_value=True))
            dve.sem_inc(peaks_moved, 1)
            dve.wait_ge(peaks_moved, 2)
            then(dve.tensor_reduce(peak_t[:, :], small_ps[0:3, 256:384], AX.X, ALU.max))
            then(dve.tensor_scalar(peak_diag[:, :], ident2[0:3, 0:3], peak_t[:, :], None, ALU.mult))
            dve.sem_inc(peaks_moved, 1)
            dve.wait_ge(peaks_moved, 4)
            then(dve.tensor_copy(peak_e[:, :], small_ps[:, 384:387]))
            then(dve.scalar_tensor_tensor(out=peak_e[:, 2:3], in0=peak_e[:, 0:1], scalar=float(D), in1=peak_e[:, 2:3], op0=ALU.mult, op1=ALU.add))
            then(dve.tensor_scalar(exponent[:, 0], peak_e[:, :].bitcast(I32), 23, None, ALU.arith_shift_right))
            then(dve.tensor_scalar(exponent[:, 1], exponent[:, 0], -1.0, 268.0, ALU.mult, ALU.add))
            then(dve.tensor_scalar(exponent[:, 2], exponent[:, 1], 186.0, None, ALU.min))
            then(dve.tensor_scalar(exponent[:, 3], exponent[:, 2], -1.0, 254.0, ALU.mult, ALU.add))
            then(dve.tensor_scalar(scale_i[:, :, :], exponent[:, 2:4], float(2 ** 23), None, ALU.mult))
            dve.tensor_scalar(undo[:, 0:1], inverse[:, 0:1], 1.0 / X_SCALE, None, ALU.mult)
            dve.tensor_copy(b1_sb[:, :, :], small_ps[:, 448:512].rearrange("p (e c) -> p e c", e=E))
            then(dve.tensor_tensor(undo[:, 1:2], inverse[:, 1:2], inverse[:, 2:3], ALU.mult))
            dve.sem_inc(scales_ready, 1)
            then(dve.tensor_copy(top_f[L, :, :], top_i[L, :, 0:TOPK].rearrange("p b k -> p k b")))
            for e in range(E):
                last = dve.tensor_scalar(onehot[L, e], top_f[L, :, :], float(e), None, ALU.is_equal)
            then(last)
            dve.tensor_tensor(member[L, :, :], onehot[L, :, 0], onehot[L, :, 1], ALU.add).then_inc(counted, 1)
            split_low(4)
            dve.wait_ge(counted, 2)
            flat = lambda a: a.rearrange("p e b -> p (e b)")
            then(dve.tensor_copy(flat(total[L, :, :]), small_ps[L, E * NB:2 * E * NB]))
            then(dve.tensor_reduce(count_f[L, :], total[L, :, :], AX.X, ALU.add))
            then(dve.tensor_scalar(count_i[L, 0], count_f[L, :], ROWS - 1.0, None, ALU.add))
            then(dve.tensor_scalar(count_i[L, 1], count_i[L, 0], 8, None, ALU.arith_shift_right))
            then(dve.tensor_copy(tiles_f[L, :], count_i[L, 1]))
            then(dve.tensor_tensor_scan(tile_end[L, :], ones[L, 0:E], tiles_f[L, :], 0.0, ALU.mult, ALU.add))
            then(dve.tensor_tensor(slot_start[L, :], tile_end[L, :], tiles_f[L, :], ALU.subtract))
            then(dve.tensor_scalar(slot_start[L, :], slot_start[L, :], float(ROWS), None, ALU.mult))
            for e in range(E):
                last = dve.tensor_tensor_scan(slot[L, e], ones[L, 0:NB], total[L, e], slot_start[L, e:e + 1], ALU.mult, ALU.add)
            then(last)
            then(dve.tensor_tensor(slot[L, :, :], slot[L, :, :], total[L, :, :], ALU.subtract))
            then(dve.tensor_tensor(flat(slot[L, :, :]), flat(slot[L, :, :]), small_ps[L, 0:E * NB], ALU.add))
            split_low(8)
            for k in range(TOPK):
                last = dve.tensor_tensor(picked[L, k], slot[L, :, :], onehot[L, :, k], ALU.mult)
            then(last)
            for k in range(TOPK):
                last = dve.tensor_reduce(slot_f[L, k], picked[L, k].rearrange("p e b -> p b e"), AX.X, ALU.add)
            then(last)
            then(dve.tensor_copy(slot_i[L, :, :], slot_f[L, :, :]))
            then(dve.tensor_scalar(high_i[L, :, :], slot_i[L, :, :], 7, None, ALU.arith_shift_right))
            then(dve.tensor_copy(high_f[L, :, :], high_i[L, :, :]))
            then(dve.scalar_tensor_tensor(out=low_f[L, :, :], in0=high_f[L, :, :], scalar=-128.0, in1=slot_f[L, :, :], op0=ALU.mult, op1=ALU.add))
            dve.wait_ge(made, 8)
            for k in range(TOPK):
                dve.tensor_tensor(high_hot[L, k], columns[L, None, 0:N_HALF].broadcast_to((LQ, NB, N_HALF)),
                                  high_f[L, k, :, None].broadcast_to((LQ, NB, N_HALF)), ALU.is_equal).then_inc(highs_hot, 1)
            for k in range(TOPK):
                for b in range(0, NB, NB // 2):
                    split_low(14 + 2 * (2 * k + b // (NB // 2)))
                    dve.tensor_tensor(low_hot[L, k, b:b + NB // 2], columns[L, None, :].broadcast_to((LQ, NB // 2, 128)),
                                      low_f[L, k, b:b + NB // 2, None].broadcast_to((LQ, NB // 2, 128)), ALU.is_equal).then_inc(lows_ready, 1)
            split_low(20)
            for e in range(E - 1):
                if e == 0:
                    then(dve.tensor_scalar(tile_acc[:, 0], tile_no[:, :], tile_end[0:1, 0:1], None, ALU.is_ge))
                else:
                    then(dve.scalar_tensor_tensor(out=tile_acc[:, e % 2], in0=tile_no[:, :], scalar=tile_end[0:1, e:e + 1], in1=tile_acc[:, (e - 1) % 2],
                                                  op0=ALU.is_ge, op1=ALU.add))
            then(dve.tensor_copy(tile_expert[:, :], tile_acc[:, (E - 2) % 2]))
            dve.sem_inc(slots_ready, 1)
            split_low(UNIT_COUNT - 8)
            dve.wait_ge(tokens_counted, 1)
            n_ = lambda n: token_f[:, n]
            then(dve.tensor_copy(token_f[:, 0:4], small_ps[:, 0:4 * N_HALF].rearrange("p (n s) -> p n s", n=4)))
            dve.tensor_tensor(n_(4), n_(1), n_(3), ALU.add)
            dve.tensor_tensor(n_(5), n_(2), n_(3), ALU.add)
            then(dve.tensor_tensor(n_(6), n_(0), n_(1), ALU.add))
            dve.tensor_tensor(n_(2), n_(6), n_(5), ALU.add)
            dve.tensor_scalar(n_(0), n_(4), 0.0, float(NB // 2 * LQ), ALU.is_gt, ALU.mult)
            then(dve.tensor_scalar(n_(1), n_(5), 0.0, float(NB * LQ), ALU.is_gt, ALU.mult))
            dve.tensor_tensor(n_(3), n_(0), n_(2), ALU.add)
            then(dve.scalar_tensor_tensor(out=n_(4), in0=n_(2), scalar=0.0, in1=spare_row[:, :], op0=ALU.is_equal, op1=ALU.mult))
            dve.tensor_scalar(token_i[:, :], n_(3), -1.0, 0.0, ALU.add, ALU.max)
            dve.tensor_tensor(n_(5), n_(1), n_(4), ALU.add)
            then(dve.tensor_scalar(n_(6), n_(3), -1.0, None, ALU.add))
            then(dve.tensor_tensor(y_row_i[:, :], n_(5), n_(6), ALU.add))
            dve.sem_inc(tokens_ready, 1)
            split_low(UNIT_COUNT)
            dve.wait_ge(b_loaded, 32)

            def split_hidden(t, m):
                s = (t.at + 1) % 2
                dve.wait_ge(gelu_done, t(4, 4 + m + 1))
                if t.at >= 1:
                    dve.wait_ge(y_done, t(1))
                dve.tensor_scalar(g_hi[:, s, m], g_sb[:, m % 2], scale[:, 2:3], None, ALU.mult).then_inc(g_high, 1)
                dve.wait_ge(g_high, t(4, 4 + m + 1))
                dve.scalar_tensor_tensor(out=g_lo[:, s, m], in0=g_sb[:, m % 2], scalar=scale[:, 2:3], in1=g_hi[:, s, m], op0=ALU.mult, op1=ALU.subtract).then_inc(g_ready, 1)

            def body(t):
                if t.has(1):
                    for m in range(3):
                        split_hidden(t, m)
                if t.has(2):
                    s = t.at % 2
                    dve.wait_ge(xt_done, t(1, 3))
                    rows = xt_ps[:, :].rearrange("p (k t) -> p k t", k=KD)
                    if t.at >= 0:
                        dve.wait_ge(h_done, t(4, 4))
                    dve.tensor_scalar(xt_hi[:, s], rows, X_SCALE, None, ALU.mult).then_inc(xt_high, 1)
                    dve.wait_ge(xt_high, t(1, 3))
                    dve.scalar_tensor_tensor(out=xt_lo[:, s], in0=rows, scalar=X_SCALE, in1=xt_hi[:, s], op0=ALU.mult, op1=ALU.subtract).then_inc(xt_copied, 1)
                if t.has(1):
                    split_hidden(t, 3)
                if t.has(0):
                    e0 = expert(dve, t, 0)
                    dve.wait_ge(y_done, t(1, 1))
                    if t.at >= 2:
                        dve.wait_ge(y_stored[t.at % 2], t.halves(32, -2))
                    dve.scalar_tensor_tensor(out=y_sb[:, t.at % 2], in0=y_ps[t.at % 2][:, :].rearrange("p (a d) -> p a d", a=2), scalar=undo[:, 1:2],
                                             in1=b2_sb[:, bass.ds(e0, 1), :].broadcast_to((128, 2, D)), op0=ALU.mult, op1=ALU.add).then_inc(y_ready, 1)

            tiles(dve, body)
            for b in range(NB):
                g, n = b // GB, b % GB
                s = g % NG
                dve.wait_ge(y_loaded[s], (g // NG + 1) * 32)
                dve.wait_ge(x2_loaded[s], (g // NG + 1) * 16)
                dve.scalar_tensor_tensor(out=x2_sb[L, s, n], in0=y_in[L, s, 0, n], scalar=weight[L, 0, b:b + 1], in1=x2_sb[L, s, n], op0=ALU.mult, op1=ALU.add).then_inc(part_done, 1)
                dve.wait_ge(part_done, b + 1)
                if g >= NG:
                    dve.wait_ge(out_stored[s], g // NG * 16)
                dve.scalar_tensor_tensor(out=o_sb[L, s, n], in0=y_in[L, s, 1, n], scalar=weight[L, 1, b:b + 1], in1=x2_sb[L, s, n], op0=ALU.mult, op1=ALU.add).then_inc(out_ready, 1)

        @block.tensor
        def _(pe):
            pe.wait_ge(made, 5)
            pe.wait_ge(peaks_moved, 1)
            nc.tensor.transpose(small_ps[0:3, 256:384], peak[:, :], ident2[:, :])
            nc.tensor.transpose(small_ps[:, 448:512], b1_rows[:, :], ident2[0:E * KF, 0:E * KF]).then_inc(peaks_moved, 1)
            pe.wait_ge(peaks_moved, 3)
            nc.tensor.matmul(small_ps[:, 384:387], ones[0:3, :], peak_diag[:, :], start=True, stop=True).then_inc(peaks_moved, 1)
            pe.wait_ge(counted, 1)
            rows = member[0:LQ, :, :].rearrange("p e b -> p (e b)")
            nc.tensor.matmul(small_ps[0:LQ, 0:E * NB], before_me[0:LQ, 0:LQ], rows, start=True, stop=True)
            nc.tensor.matmul(small_ps[0:LQ, E * NB:2 * E * NB], ones[0:LQ, 0:LQ], rows, start=True, stop=True).then_inc(counted, 1)
            for k in range(TOPK):
                for h in range(2):
                    pe.wait_ge(highs_ready, k + 1)
                    pe.wait_ge(lows_ready, 2 * k + h + 1)
                    n = 2 * k + h
                    for b in range(NB // 2):
                        last = nc.tensor.matmul(small_ps[:, n * N_HALF:(n + 1) * N_HALF], low_hot[0:LQ, k, h * NB // 2 + b], high_hot[0:LQ, k, h * NB // 2 + b],
                                                start=(b == 0), stop=(b == NB // 2 - 1))
            last.then_inc(tokens_counted, 1)
            pe.wait_ge(slots_ready, 1)
            pe.wait_ge(w_split, UNIT_COUNT // 4 * 3)
            pe.wait_ge(w_split_pool, UNIT_COUNT // 4)
            PARTS = ((0, 0), (0, 1), (1, 0))

            def body(t):
                if t.has(1):
                    e1 = expert(pe, t, 1)
                    s1 = (t.at + 1) % 2
                    pe.wait_ge(xt_copied, t(1, 2))
                    for m in range(4):
                        if t.at >= 0:
                            pe.wait_ge(gelu_done, t(4, m + 1))
                        for c in range(2):
                            f = (m * 2 + c) * 128
                            for k in range(KD):
                                for n, (a, b) in enumerate(PARTS):
                                    last = nc.tensor.matmul(h_ps[m][:, c * ROWS:c * ROWS + ROWS], (w1_hi, w1_lo)[a][:, k, bass.ds(e1, 1), f:f + 128].rearrange("p o f -> p (o f)"),
                                                            (xt_hi, xt_lo)[b][:, s1, k], start=(k == n == 0), stop=(k == KD - 1 and n == 2))
                        last.then_inc(h_done, 1)
                if t.has(2):
                    pe.wait_ge(x_loaded[t.at % 2], t.halves(32, 2))
                    if t.at >= -1:
                        pe.wait_ge(xt_copied, t(1, 2))
                    for k in range(KD):
                        for a in range(2):
                            last = nc.tensor.transpose(xt_ps[:, k * ROWS + a * 128:k * ROWS + a * 128 + 128], x_sb[:, t.at % 2, a, k * 128:k * 128 + 128], ident2[:, :])
                    last.then_inc(xt_done, 1)
                if t.has(0):
                    e0 = expert(pe, t, 0)
                    s = t.at % 2
                    if t.at >= 2:
                        pe.wait_ge(y_ready, t(1, -1))
                    for r in range(2):
                        for m in range(4):
                            if r == 0:
                                pe.wait_ge(g_ready, t(4, m + 1))
                            for c in range(2):
                                for n, (a, b) in enumerate(PARTS):
                                    last = nc.tensor.matmul(y_ps[s][:, r * D:r * D + D], (g_hi, g_lo)[a][:, s, m, c, r * 128:r * 128 + 128],
                                                            (w2_hi, w2_lo)[b][:, m * 2 + c, bass.ds(e0, 1), :].rearrange("p o d -> p (o d)"),
                                                            start=(m == c == n == 0), stop=(m == 3 and c == 1 and n == 2))
                    last.then_inc(y_done, 1)

            tiles(pe, body)


def program(nc, x, ctx, g_x, g_f, ln_m_g, ln_m_b, ln_l_g, ln_l_b, wq, wkv, wout, gate_w, w1, b1, w2, b2, out):
    dram = lambda name, shape: nc.dram_tensor(name, shape, F32).ap()
    x2_dram = dram("x2_dram", [NB, LQ, D])
    xn_dram = dram("xn_dram", [NB, LQ, D])
    y_rows = dram("y_rows", [TOPK * NB * LQ + TILES * ROWS, D])
    with ExitStack() as st:
        top_v = st.enter_context(nc.sbuf_tensor("top_v", [128, NB, TOPK], F32))
        top_i = st.enter_context(nc.sbuf_tensor("top_i", [128, NB, TOPK], U32))
        peaks = st.enter_context(nc.sbuf_tensor("peaks", [128, NB, 2], F32))
        with ExitStack() as inner:
            ident = inner.enter_context(nc.sbuf_tensor("ident", [128, 128], F32))
            attention(nc, x, ctx, g_x, ln_m_g, ln_m_b, ln_l_g, ln_l_b, wq, wkv, wout, gate_w, x2_dram, xn_dram, top_v, top_i, ident, w1, w2, peaks)
        routed_ffn(nc, g_f, w1, b1, w2, b2, x2_dram, xn_dram, out, y_rows, top_v, top_i, peaks)


_INS = ['x', 'ctx_1024', 'g_xattn', 'g_ffn', 'L0_xattn_ln_m_g', 'L0_xattn_ln_m_b', 'L0_xattn_ln_l_g', 'L0_xattn_ln_l_b',
        'L0_xattn_Wq', 'L0_xattn_Wkv', 'L0_xattn_Wout', 'L0_ffn_gate_w', 'L0_ffn_w1', 'L0_ffn_b1', 'L0_ffn_w2', 'L0_ffn_b2']
_OUTS = [((NB, LQ, D), 'float32')]


def kernel(**inputs):
    import numpy as _np
    import concourse.bacc as _bacc
    from concourse import mybir as _mybir
    from concourse.bass_utils import run_bass_kernel_spmd as _run

    nc = _bacc.Bacc("TRN2", target_bir_lowering=False, num_devices=1)
    arrays, args = {}, []
    for name in _INS:
        a = _np.ascontiguousarray(inputs[name])
        arrays[f"in_{name}_dram"] = a
        args.append(nc.dram_tensor(f"in_{name}_dram", a.shape, _mybir.dt.from_np(a.dtype), kind="ExternalInput").ap())
    for i, (shape, dtype) in enumerate(_OUTS):
        dt = _mybir.dt.from_np(_np.dtype(dtype))
        args.append(nc.dram_tensor(f"out_{i}_dram", shape, dt, kind="ExternalOutput").ap())
    program(nc, *args)
    r = _run(nc, [arrays], core_ids=[0])
    got = tuple(r.results[0][f"out_{i}_dram"] for i in range(len(_OUTS)))
    return got[0]
```
